# Optimizing a Trainium2 kernel written in Bass

```python
import numpy as np
import jax
import jax.numpy as jnp

def _softmax(x, axis=-1):
    return jax.nn.softmax(x, axis=axis)

def _gelu(x):
    return jax.nn.gelu(x, approximate=True)

def _silu(x):
    return jax.nn.silu(x)

def _sigmoid(x):
    return jax.nn.sigmoid(x)

def _layernorm(x, axis=-1, eps=1e-05):
    m = jnp.mean(x, axis=axis, keepdims=True)
    v = jnp.var(x, axis=axis, keepdims=True)
    return (x - m) / jnp.sqrt(v + eps)

def _scatter_add(tgt, idx, src, axis=0):
    return tgt.at[idx].add(src)

def _segment_sum(src, seg, n):
    return jax.ops.segment_sum(src, seg, n)
kernel_name = 'mk_gps_d1_gnn_r16_6ddc1e'

def setup_inputs(seed: int=0):
    np.random.seed(seed)
    _w = jnp.asarray

    def _rec_inputs():
        import jax
        import jax.numpy as jnp
        _gk = jax.random.key(seed)
        x = -0.0006008 + 1.001 * jax.random.normal(jax.random.fold_in(_gk, 1), (6250, 256), jnp.float32)
        src = jax.random.randint(jax.random.fold_in(_gk, 2), (100000,), 0, 6250, jnp.int32)
        dst = jnp.minimum((6250 * jax.random.uniform(jax.random.fold_in(_gk, 3), (100000,)) ** 2.0).astype(jnp.int32), 99999)
        _o = jnp.argsort(dst, stable=True)
        src = src[_o]
        dst = dst[_o]
        return (x, src, dst)
    x, src, dst = _rec_inputs()

    def _L0_gnn_setup():
        import jax, jax.numpy as jnp
        import numpy as np
        N, E, D = (625, 20000, 256)

        def _add_self_loops(src, dst, n):
            loop = jnp.arange(n, dtype=src.dtype)
            return (jnp.concatenate([src, loop]), jnp.concatenate([dst, loop]))

        def _gcn_conv(x, W, b, src, dst, n):
            xw = x @ W
            deg = jax.ops.segment_sum(jnp.ones(src.shape[0], x.dtype), dst, num_segments=n)
            dinv = jnp.where(deg > 0, jax.lax.rsqrt(deg), 0.0)
            norm = dinv[src] * dinv[dst]
            agg = jax.ops.segment_sum(xw[src] * norm[:, None], dst, num_segments=n)
            return agg + b

        def _gat_conv(x, W, a_src, a_dst, b, src, dst, n):
            xw = x @ W
            e = jax.nn.leaky_relu((xw @ a_src)[src] + (xw @ a_dst)[dst], 0.2)
            m = jax.ops.segment_max(e, dst, num_segments=n)
            ex = jnp.exp(e - m[dst])
            s = jax.ops.segment_sum(ex, dst, num_segments=n)
            alpha = ex / (s[dst] + 1e-16)
            agg = jax.ops.segment_sum(alpha[:, None] * xw[src], dst, num_segments=n)
            return agg + b
        key = jax.random.key(seed)
        ks = jax.random.split(key, 6)
        return {'event_emb': jax.random.normal(ks[0], (N, D), jnp.float32), 'edge_index': jax.random.randint(ks[1], (2, E), 0, N), 'W1': jax.random.normal(ks[2], (D, D), jnp.float32) / np.sqrt(D).astype(np.float32), 'b1': jnp.zeros((D,), jnp.float32), 'W2': jax.random.normal(ks[3], (D, D), jnp.float32) / np.sqrt(D).astype(np.float32), 'att_src': jax.random.normal(ks[4], (D,), jnp.float32) / np.sqrt(D).astype(np.float32), 'att_dst': jax.random.normal(ks[5], (D,), jnp.float32) / np.sqrt(D).astype(np.float32), 'b2': jnp.zeros((D,), jnp.float32)}
    _L0_gnn_all = _L0_gnn_setup()
    _L0_gnn_in = {k: v for k, v in _L0_gnn_all.items() if k in ('W1', 'b1', 'W2', 'att_src', 'att_dst', 'b2')}
    del _L0_gnn_all

    def _L0_mix_setup():
        import jax, jax.numpy as jnp
        import numpy as np
        HEADS, DIM_HEAD = (8, 64)
        EPS = 1e-05

        def instance_norm(t):
            mu = jnp.mean(t, axis=-1, keepdims=True)
            var = jnp.mean((t - mu) ** 2, axis=-1, keepdims=True)
            return (t - mu) * jax.lax.rsqrt(var + EPS)
        key = jax.random.key(seed)
        k1, k2, k3, k4 = jax.random.split(key, 4)
        B, N, D = (8, 512, 256)
        inner = HEADS * DIM_HEAD
        x = jax.random.normal(k1, (B, N, D), jnp.float32)
        w_qkv = jax.random.normal(k2, (3 * inner, D), jnp.float32) / np.sqrt(D).astype(np.float32)
        w_out = jax.random.normal(k3, (D, inner), jnp.float32) / np.sqrt(inner).astype(np.float32)
        b_out = 0.01 * jax.random.normal(k4, (D,), jnp.float32)
        return {'x': x, 'w_qkv': w_qkv, 'w_out': w_out, 'b_out': b_out}
    _L0_mix_all = _L0_mix_setup()
    _L0_mix_in = {k: v for k, v in _L0_mix_all.items() if k in ('w_qkv', 'w_out', 'b_out')}
    del _L0_mix_all

    def _L0_ffn_setup():
        import jax, jax.numpy as jnp
        import numpy as np
        B, S, D, E, H, K = (4, 256, 256, 8, 512, 2)
        key = jax.random.key(seed)
        ks = jax.random.split(key, 6)
        x = jax.random.normal(ks[0], (B, S, D), jnp.float32)
        Wg = jax.random.normal(ks[1], (D, E), jnp.float32) * 0.02
        bg = jnp.zeros((E,), jnp.float32)
        W1 = jax.random.normal(ks[2], (E, D, H), jnp.float32) * 0.02
        b1 = jnp.zeros((E, H), jnp.float32)
        W2 = jax.random.normal(ks[3], (E, H, D), jnp.float32) * 0.02
        b2 = jnp.zeros((E, D), jnp.float32)
        return {'x': x, 'Wg': Wg, 'bg': bg, 'W1': W1, 'b1': b1, 'W2': W2, 'b2': b2}
    _L0_ffn_all = _L0_ffn_setup()
    _L0_ffn_in = {k: v for k, v in _L0_ffn_all.items() if k in ('Wg', 'bg', 'W1', 'b1', 'W2', 'b2')}
    del _L0_ffn_all
    return {'x': x, 'src': src, 'dst': dst, 'L0_gnn_W1': _L0_gnn_in['W1'], 'L0_gnn_b1': _L0_gnn_in['b1'], 'L0_gnn_W2': _L0_gnn_in['W2'], 'L0_gnn_att_src': _L0_gnn_in['att_src'], 'L0_gnn_att_dst': _L0_gnn_in['att_dst'], 'L0_gnn_b2': _L0_gnn_in['b2'], 'L0_mix_w_qkv': _L0_mix_in['w_qkv'], 'L0_mix_w_out': _L0_mix_in['w_out'], 'L0_mix_b_out': _L0_mix_in['b_out'], 'L0_ffn_Wg': _L0_ffn_in['Wg'], 'L0_ffn_bg': _L0_ffn_in['bg'], 'L0_ffn_W1': _L0_ffn_in['W1'], 'L0_ffn_b1': _L0_ffn_in['b1'], 'L0_ffn_W2': _L0_ffn_in['W2'], 'L0_ffn_b2': _L0_ffn_in['b2']}

def reference(x, src, dst, L0_gnn_W1, L0_gnn_b1, L0_gnn_W2, L0_gnn_att_src, L0_gnn_att_dst, L0_gnn_b2, L0_mix_w_qkv, L0_mix_w_out, L0_mix_b_out, L0_ffn_Wg, L0_ffn_bg, L0_ffn_W1, L0_ffn_b1, L0_ffn_W2, L0_ffn_b2):
    import jax
    import jax.numpy as jnp

    def _L0_gnn_ref(event_emb, edge_index, W1, b1, W2, att_src, att_dst, b2):
        import jax, jax.numpy as jnp
        import numpy as np
        N, E, D = (625, 20000, 256)

        def _add_self_loops(src, dst, n):
            loop = jnp.arange(n, dtype=src.dtype)
            return (jnp.concatenate([src, loop]), jnp.concatenate([dst, loop]))

        def _gcn_conv(x, W, b, src, dst, n):
            xw = x @ W
            deg = jax.ops.segment_sum(jnp.ones(src.shape[0], x.dtype), dst, num_segments=n)
            dinv = jnp.where(deg > 0, jax.lax.rsqrt(deg), 0.0)
            norm = dinv[src] * dinv[dst]
            agg = jax.ops.segment_sum(xw[src] * norm[:, None], dst, num_segments=n)
            return agg + b

        def _gat_conv(x, W, a_src, a_dst, b, src, dst, n):
            xw = x @ W
            e = jax.nn.leaky_relu((xw @ a_src)[src] + (xw @ a_dst)[dst], 0.2)
            m = jax.ops.segment_max(e, dst, num_segments=n)
            ex = jnp.exp(e - m[dst])
            s = jax.ops.segment_sum(ex, dst, num_segments=n)
            alpha = ex / (s[dst] + 1e-16)
            agg = jax.ops.segment_sum(alpha[:, None] * xw[src], dst, num_segments=n)
            return agg + b
        n = event_emb.shape[0]
        src, dst = _add_self_loops(edge_index[0], edge_index[1], n)
        x = jax.nn.relu(_gcn_conv(event_emb, W1, b1, src, dst, n))
        x = jax.nn.relu(_gat_conv(x, W2, att_src, att_dst, b2, src, dst, n))
        return x

    def _L0_mix_ref(x, w_qkv, w_out, b_out):
        import jax, jax.numpy as jnp
        import numpy as np
        HEADS, DIM_HEAD = (8, 64)
        EPS = 1e-05

        def instance_norm(t):
            mu = jnp.mean(t, axis=-1, keepdims=True)
            var = jnp.mean((t - mu) ** 2, axis=-1, keepdims=True)
            return (t - mu) * jax.lax.rsqrt(var + EPS)
        B, N, _ = x.shape
        H, Dh = (HEADS, DIM_HEAD)
        qkv = jnp.einsum('bnd,ed->bne', x, w_qkv)
        q, k, v = jnp.split(qkv, 3, axis=-1)

        def to_heads(t):
            return t.reshape(B, N, H, Dh).transpose(0, 2, 1, 3)
        q, k, v = (to_heads(q), to_heads(k), to_heads(v))
        k = instance_norm(k)
        v = instance_norm(v)
        dots = jnp.einsum('bhnd,bhne->bhde', k, v)
        out = jnp.einsum('bhnd,bhde->bhne', q, dots) / N
        out = out.transpose(0, 2, 1, 3).reshape(B, N, H * Dh)
        return jnp.einsum('bne,de->bnd', out, w_out) + b_out

    def _L0_ffn_ref(x, Wg, bg, W1, b1, W2, b2):
        import jax, jax.numpy as jnp
        import numpy as np
        B, S, D, E, H, K = (4, 256, 256, 8, 512, 2)
        Bv, Sv, Dv = x.shape
        gate_scores = x @ Wg + bg
        _, idx = jax.lax.top_k(gate_scores, K)
        mask = jax.nn.one_hot(idx, E, dtype=x.dtype).sum(axis=-2)
        xf = x.reshape(-1, Dv)
        mf = mask.reshape(-1, E)
        h = jax.nn.gelu(jnp.einsum('td,edh->teh', xf, W1) + b1[None], approximate=False)
        y = jnp.einsum('teh,ehd->ted', h, W2) + b2[None]
        out = jnp.einsum('ted,te->td', y, mf)
        return out.reshape(Bv, Sv, Dv)
    edge_index = jnp.stack([src, dst])
    xn = _layernorm(x, axis=-1)
    x = x + _L0_gnn_ref(xn, edge_index, L0_gnn_W1, L0_gnn_b1, L0_gnn_W2, L0_gnn_att_src, L0_gnn_att_dst, L0_gnn_b2) + _L0_mix_ref(xn[None], L0_mix_w_qkv, L0_mix_w_out, L0_mix_b_out)[0]
    x = x + _L0_ffn_ref(_layernorm(x, axis=-1)[None], L0_ffn_Wg, L0_ffn_bg, L0_ffn_W1, L0_ffn_b1, L0_ffn_W2, L0_ffn_b2)[0]
    return x

_drawn_inputs = setup_inputs


def setup_inputs(seed=0):
    import zlib

    import numpy as np

    out = dict(_drawn_inputs(seed))
    spreads = {'L0_gnn_b1': (0.0, 0.1),
     'L0_gnn_b2': (0.0, 0.1),
     'L0_ffn_bg': (0.0, 0.1),
     'L0_ffn_b1': (0.0, 0.1),
     'L0_ffn_b2': (0.0, 0.1)}
    factors = {'L0_gnn_att_src': 7.755, 'L0_gnn_att_dst': 76.929, 'L0_mix_b_out': 4.121}
    for name, (base, spread) in spreads.items():
        noise = np.random.default_rng([zlib.crc32(name.encode()), seed]).standard_normal(out[name].shape)
        drawn = base * np.exp(spread * noise) if base else spread * noise
        out[name] = jnp.asarray(drawn.astype(out[name].dtype))
    for name, factor in factors.items():
        out[name] = (out[name] * factor).astype(out[name].dtype)
    return out
```

```python
import concourse.bass as bass
from concourse import mybir
from contextlib import ExitStack

F32 = mybir.dt.float32
BF16 = mybir.dt.bfloat16
I32 = mybir.dt.int32
ALU = mybir.AluOpType
ACT = mybir.ActivationFunctionType
AX = mybir.AxisListType

P = 128
N, D, E = 6250, 256, 100000
NB = 50
NP = NB * P
FULL = N // P
REST = N - FULL * P
TG = 7
TP = TG * P
NT = 784
GV = 8
NV = 832
NG = NV // GV
SLOTS = 4
W = D + 2
HEADS, DH = 8, 64
INNER = HEADS * DH
NE, HID = 8, 512
HC = HID // P
EPS = 1e-5
SLOPE = 0.2
BIG = 1e30
TB = 5
TT = TB * P


class Steps:

    def __init__(self, eng, sem, pace):
        self.eng, self.sem, self.pace, self.n, self.base = eng, sem, pace, 0, 0

    def add(self, ins):
        ins.then_inc(self.sem, 1)
        self.n += 1

    def last(self, plain=False):
        if self.n or not isinstance(self.base, int):
            hold(self.eng, self.sem, self.base + self.n, self.pace, plain)

    def loop(self, done, per):
        self.outer = (self.base, self.n, per)
        self.base, self.n = self.base + self.n + done * per, 0

    def end(self, bodies):
        base, n, per = self.outer
        assert self.n == per, (self.n, per)
        self.base, self.n = base, n + bodies * per


def hold(eng, sem, value, pace, plain=False):
    eng.wait_ge(sem, value)
    if not isinstance(value, int) and not plain:
        eng.sem_inc(pace, 1)


def layernorm(v, st, src, pitch, X, stats, sm, mean, rstd, act_root, root_done):
    st.last()
    with v.Fori(0, NB // TB) as i:
        for k in range(TB):
            ins = v.bn_stats(stats[:, bass.ds(i * (TB * 6) + k * 6, 6)],
                             src[:, bass.ds(i * (TB * pitch) + k * pitch, D)])
        st.loop(i, 1)
        st.add(ins)
    st.end(NB // TB)
    st.last()
    s = stats[:, :].rearrange("p (b s) -> p b s", s=6)
    m0, v0, m1, v1 = s[:, :, 1], s[:, :, 2], s[:, :, 4], s[:, :, 5]
    st.add(v.tensor_tensor(mean, m0, m1, ALU.add))
    st.add(v.tensor_tensor(rstd, m0, m1, ALU.subtract))
    st.last()
    st.add(v.tensor_scalar(mean, mean, 0.5, None, ALU.mult))
    st.add(v.scalar_tensor_tensor(sm[:, 0, :], rstd, 0.25, rstd, ALU.mult, ALU.mult))
    st.add(v.tensor_tensor(sm[:, 1, :], v0, v1, ALU.add))
    st.last()
    st.add(v.scalar_tensor_tensor(sm[:, 0, :], sm[:, 1, :], 1.0 / D, sm[:, 0, :], ALU.mult, ALU.add))
    st.last()
    v.tensor_scalar(sm[:, 0, :], sm[:, 0, :], EPS, None, ALU.add).then_inc(act_root, 1)
    v.wait_ge(root_done, 1)
    st.add(v.reciprocal(rstd, sm[:, 1, :]))
    st.last()
    with v.Fori(0, NB // TB) as i:
        for k in range(TB):
            ins = v.tensor_scalar(X[:, bass.ds(i * (TB * D) + k * D, D)],
                                  src[:, bass.ds(i * (TB * pitch) + k * pitch, D)], mean[:, bass.ds(i * TB + k, 1)], rstd[:, bass.ds(i * TB + k, 1)],
                                  ALU.subtract, ALU.mult)
        st.loop(i, 1)
        st.add(ins)
    st.end(NB // TB)
    st.last()


def node_rows(flat):
    return flat.rearrange("(b l) c -> l b c", l=P)


def program(nc, x, src, dst, gW1, gb1, gW2, att_s, att_d, gb2, w_qkv, w_out, b_out, Wg, bg, fW1, fb1, fW2, fb2, out):
    ctx = ExitStack()

    def dram(name, shape, dt=F32):
        return nc.dram_tensor(name, shape, dt, kind="Internal").ap()

    x_pad = dram("x_pad", (NP, D))
    table1 = dram("table1", (NP, D))
    table2 = dram("table2", (NP, D))
    src_rows = dram("src_rows", (TP, P), I32)
    dst_rows = dram("dst_rows", (TP, P), I32)
    ends = dram("ends", (4, TP))
    blk_row = dram("blk_row", (TP,), I32)
    low_s = dram("low_s", (TP * P,), BF16)
    low_d = dram("low_d", (TP * P,), BF16)
    w_rows = dram("w_rows", (TP, P))
    m_rows = dram("m_rows", (TP, P))
    carry_rows = dram("carry_rows", (4, TP))

    with ctx:
        def mk(stack):
            return (lambda n, s, dt=F32: stack.enter_context(nc.sbuf_tensor(n, s, dt)),
                    lambda n, s, dt=F32: stack.enter_context(nc.psum_tensor(n, s, dt)),
                    lambda n: stack.enter_context(nc.semaphore(n)))

        sb, pb, sem = mk(ctx)
        X = sb("X", [P, NB * D])
        ACC = sb("ACC", [P, NB * W])
        ident = sb("ident", [P, P])
        iota_f = sb("iota_f", [P, P])
        dinv = sb("dinv", [P, NB])
        AS = sb("AS", [P, NB])
        AD = sb("AD", [P, NB])
        eps_t = sb("eps_t", [P, 1])
        pace = {n: sem("pace_" + n) for n in ("act", "pe", "dve", "pool", "sp")}
        Xb = X[:, :].rearrange("p (b d) -> p b d", d=D)
        Ab = ACC[:, :].rearrange("p (b d) -> p b d", d=W)

        edges = ctx.enter_context(ExitStack())
        sb, pb, sem = mk(edges)
        idx = sb("idx", [P, TP], I32)
        rel = sb("rel", [P, TP])
        WE = sb("WE", [P, TP])
        ME = sb("ME", [P, TP])
        blkv = sb("blkv", [1, TP], I32)
        tvI = sb("tvI", [P, TG], I32)
        blkS = sb("blkS", [P, TP], BF16)
        blkD = sb("blkD", [P, TP], BF16)
        io_b = sb("io_b", [P, NB], BF16)

        with ExitStack() as sc:
            sb, pb, sem = mk(sc)
            stats = sb("stats", [P, NB * 6])
            sm = sb("sm", [P, 2, NB])
            mean = sb("mean", [P, NB])
            rstd = sb("rstd", [P, NB])
            sT = sb("sT", [P, TG, P], I32)
            dT = sb("dT", [P, TG, P], I32)
            dF = sb("dF", [P, TG, P])
            sF = sb("sF", [P, TG, P])
            sE = sb("sE", [P, TP], I32)
            lowI = sb("lowI", [P, TG, P], I32)
            lowsB = sb("lowsB", [P, TG, P], BF16)
            lowdB = sb("lowdB", [P, TG, P], BF16)
            endI = sb("endI", [P, 2, TG], I32)
            endF = sb("endF", [P, 4, TG])
            rows = sb("rows", [P, 2, TP])
            vs = sb("vs", [P, TP])
            dq = sb("dq", [P, TP])
            tmp = sb("tmp", [P, TP])
            tv = sb("tv", [P, TG])
            bv = sb("bv", [P, TG])
            bvI = sb("bvI", [P, TG], I32)
            viota = sb("viota", [P, TG])
            srcV = sb("srcV", [P, TG, P], I32)
            dstV = sb("dstV", [P, TG, P], I32)
            srcVf = sb("srcVf", [P, TG, P])
            dstVf = sb("dstVf", [P, TG, P])
            dE = sb("dE", [P, TP], I32)
            lowE = sb("lowE", [P, TP], BF16)
            blkEi = sb("blkEi", [P, TP], I32)
            io_l = sb("io_l", [P, P], BF16)
            OL = sb("OL", [P, 2, GV, P], BF16)
            OB = sb("OB", [P, 2, GV, NB], BF16)
            zero = sb("zero", [P, P], BF16)
            tp = [pb(f"tpA{i}", [P, 512]) for i in range(2)]
            hist = pb("hist", [P, 512])
            consts = sem("a_consts")
            padded = sem("a_padded")
            x_in = sem("a_x_in")
            e_in = sem("a_e_in")
            written = sem("a_written")
            tiles_out = sem("a_tiles_out")
            rows_in = sem("a_rows_in")
            ends_ready = sem("a_ends_ready")
            tv_ready = sem("a_tv_ready")
            bv_out = sem("a_bv_out")
            gathered = sem("a_gathered")
            vf_ready = sem("a_vf_ready")
            turned = sem("a_turned")
            copied = sem("a_copied")
            oh_ready = sem("a_oh_ready")
            oh_used = sem("a_oh_used")
            root_in = sem("a_root_in")
            root_out = sem("a_root_out")
            y_ready = sem("a_y_ready")
            steps = sem("a_steps")
            low_ready = sem("a_low_ready")
            block = sc.enter_context(nc.Block())

            @block.gpsimd
            def _(g):
                g.memset(ident[:, :], 0.0).then_inc(consts, 1)
                g.iota(iota_f[:, :], [[1, P]], base=0, channel_multiplier=0,
                       allow_small_or_imprecise_dtypes=True).then_inc(consts, 1)
                g.iota(viota[:, :], [[P, TG]], base=0, channel_multiplier=1,
                       allow_small_or_imprecise_dtypes=True).then_inc(consts, 1)
                g.memset(zero[:, :], 0.0).then_inc(consts, 1)
                g.wait_ge(consts, 4)
                g.affine_select(out=ident[:, :], in_=ident[:, :], compare_op=ALU.not_equal, fill=1.0,
                                base=0, pattern=[[-1, P]], channel_multiplier=1).then_inc(consts, 1)
                g.wait_ge(tiles_out, 32)
                g.wait_ge(tv_ready, 1)
                for k in range(TG):
                    for rows_d, to in ((src_rows, srcV), (dst_rows, dstV)):
                        g.indirect_dma_start(to[:, k, :], None, rows_d[:, :],
                                             bass.IndirectOffsetOnAxis(ap=tvI[:, k:k + 1], axis=0)
                                             ).then_inc(gathered, 16)

            @block.sync
            def _(sp):
                sp.wait_ge(padded, 4)
                body = slice(0, FULL * P)
                sp.dma_start(Xb[:, 0:FULL, :], x[body, :].rearrange("(b l) d -> l b d", l=P)).then_inc(x_in, 16)
                sp.dma_start(Xb[0:REST, FULL, :], x[FULL * P:N, :]).then_inc(x_in, 16)
                for a, to in ((src, sT), (dst, dT)):
                    whole = (TG - 1) * P * P
                    left = (E - whole) // P
                    sp.dma_start(to[:, 0:TG - 1, :], a[0:whole].rearrange("(g t p) -> t g p", p=P, t=P)).then_inc(e_in, 16)
                    sp.dma_start(to[0:left, TG - 1, :], a[whole:whole + left * P].rearrange("(t p) -> t p", p=P)).then_inc(e_in, 16)
                    sp.dma_start(to[left:left + 1, TG - 1, 0:E - whole - left * P],
                                 a[whole + left * P:E].unsqueeze(0)).then_inc(e_in, 16)
                sp.wait_ge(x_in, 32)
                sp.dma_start(node_rows(x_pad), Xb).then_inc(written, 16)
                sp.wait_ge(e_in, 96)
                sp.dma_start(src_rows.rearrange("(g t) p -> t g p", t=P), sT[:, :, :]).then_inc(tiles_out, 16)
                sp.dma_start(dst_rows.rearrange("(g t) p -> t g p", t=P), dT[:, :, :]).then_inc(tiles_out, 16)
                sp.wait_ge(ends_ready, 1)
                for k in range(4):
                    sp.dma_start(ends[k, :].rearrange("(g t) -> t g", t=P), endF[:, k, :], allow_slow_non_contiguous=True).then_inc(bv_out, 16)
                sp.wait_ge(bv_out, 64)
                for k in range(2):
                    sp.dma_start(rows[:, k, :], ends[k, :].partition_broadcast(P)).then_inc(rows_in, 16)
                sp.wait_ge(low_ready, 2)
                sp.dma_start(low_s.rearrange("(g t p) -> t g p", t=P, p=P), lowsB[:, :, :]).then_inc(written, 16)
                sp.dma_start(low_d.rearrange("(g t p) -> t g p", t=P, p=P), lowdB[:, :, :]).then_inc(written, 16)
                sp.wait_ge(tv_ready, 2)
                sp.dma_start(blk_row.rearrange("(g t) -> t g", t=P), bvI[:, :], allow_slow_non_contiguous=True).then_inc(bv_out, 16)
                sp.wait_ge(bv_out, 80)
                sp.dma_start(blkv[:, :], blk_row.unsqueeze(0)).then_inc(bv_out, 16)
                sp.wait_ge(y_ready, 1)
                sp.dma_start(node_rows(table1), Ab[:, :, 0:D]).then_inc(written, 16)
                sp.wait_ge(written, 64)
                sp.wait_ge(bv_out, 96)

            @block.scalar
            def _(a):
                a.wait_ge(root_in, 1)
                a.activation(sm[:, 1, :], sm[:, 0, :], ACT.Sqrt).then_inc(root_out, 1)
                a.wait_ge(root_in, 2)
                a.activation(sm[:, 1, :], sm[:, 0, :], ACT.Sqrt).then_inc(root_out, 1)

            @block.tensor
            def _(t):
                t.wait_ge(consts, 5)
                t.wait_ge(vf_ready, 1)
                for n in range(2 * TG):
                    if n >= 2:
                        t.wait_ge(copied, n - 1)
                    part = dF if n < TG else sF
                    t.transpose(tp[n % 2][:, 0:P], part[:, n % TG, :], ident[:, :]).then_inc(turned, 1)
                t.matmul(hist[:, 0:NB], zero[:, :], zero[:, 0:NB], start=True, stop=False)
                with t.Fori(0, NT // GV // 2) as i:
                    for h in range(2):
                        t.wait_ge(oh_ready, i * 2 + h + 1)
                        for k in range(GV):
                            mm = t.matmul(hist[:, 0:NB], OL[:, h, k, :], OB[:, h, k, :], start=False, stop=False)
                        mm.then_inc(oh_used, 1)
                t.matmul(hist[:, 0:NB], zero[:, :], zero[:, 0:NB], start=False, stop=True
                         ).then_inc(oh_used, 1)
                t.wait_ge(vf_ready, 3)
                for n in range(2 * TG):
                    part = dstVf if n < TG else srcVf
                    t.wait_ge(copied, 2 * TG + n - 1)
                    t.transpose(tp[n % 2][:, 0:P], part[:, n % TG, :], ident[:, :]).then_inc(turned, 1)

            @block.vector
            def _(v):
                st = Steps(v, steps, pace["dve"])
                v.memset(Xb[:, FULL:NB, :], 0.0).then_inc(padded, 1)
                v.memset(sT[:, TG - 1, :], 0).then_inc(padded, 1)
                v.memset(dT[:, TG - 1, :], NP - 1).then_inc(padded, 1)
                v.memset(eps_t[:, :], EPS).then_inc(padded, 1)
                st.add(v.memset(Ab[:, :, D:W], 0.0))
                v.wait_ge(e_in, 96)
                st.add(v.tensor_copy(dF[:, :, :], dT[:, :, :]))
                st.last()
                st.add(v.tensor_copy(endF[:, 2, :], dF[:, :, 0]))
                st.add(v.tensor_copy(sF[:, :, :], sT[:, :, :]))
                st.last()
                v.tensor_copy(endF[:, 3, :], dF[:, :, P - 1]).then_inc(vf_ready, 1)
                st.add(v.tensor_scalar(endI[:, 0, :], dT[:, :, 0], 7, None, ALU.arith_shift_right))
                st.add(v.tensor_scalar(endI[:, 1, :], dT[:, :, P - 1], 7, None, ALU.arith_shift_right))
                st.last()
                v.tensor_copy(endF[:, 0:2, :], endI[:, :, :]).then_inc(ends_ready, 1)
                st.add(v.tensor_scalar(lowI[:, :, :], sT[:, :, :], P - 1, None, ALU.bitwise_and))
                st.last()
                st.add(v.tensor_copy(lowsB[:, :, :], lowI[:, :, :]))
                st.last()
                v.sem_inc(low_ready, 1)
                st.add(v.tensor_scalar(lowI[:, :, :], dT[:, :, :], P - 1, None, ALU.bitwise_and))
                st.last()
                v.tensor_copy(lowdB[:, :, :], lowI[:, :, :]).then_inc(low_ready, 1)
                for n in range(2 * TG):
                    v.wait_ge(turned, n + 1)
                    to = (dE if n < TG else sE)[:, (n % TG) * P:(n % TG + 1) * P]
                    v.tensor_copy(to, tp[n % 2][:, 0:P]).then_inc(copied, 1)
                v.wait_ge(copied, 2 * TG)
                v.wait_ge(consts, 5)
                st.add(v.tensor_scalar(blkEi[:, :], dE[:, :], 7, None, ALU.arith_shift_right))
                st.add(v.tensor_scalar(dE[:, :], dE[:, :], P - 1, None, ALU.bitwise_and))
                st.add(v.tensor_copy(io_l[:, :], iota_f[:, :]))
                st.add(v.tensor_copy(io_b[:, :], iota_f[:, 0:NB]))
                st.last()
                st.add(v.tensor_copy(lowE[:, :], dE[:, :]))
                st.add(v.tensor_copy(blkD[:, :], blkEi[:, :]))
                st.add(v.tensor_scalar(sE[:, :], sE[:, :], 7, None, ALU.arith_shift_right))
                st.last()
                st.add(v.tensor_copy(blkS[:, :], sE[:, :]))

                v.wait_ge(rows_in, 32)
                st.add(v.tensor_tensor(tmp[:, :], rows[:, 1, :], rows[:, 0, :], ALU.subtract))
                st.last()
                st.add(v.tensor_scalar(tmp[:, :], tmp[:, :], 1.0, None, ALU.add))
                st.last()
                st.add(v.memset(dq[:, :], 0.0))
                st.last()
                st.add(v.tensor_tensor_scan(vs[:, :], tmp[:, :], dq[:, :], 0.0, ALU.add, ALU.add))
                st.last()
                st.add(v.tensor_tensor(vs[:, :], vs[:, :], tmp[:, :], ALU.subtract))
                st.last()
                st.add(v.tensor_tensor(tmp[:, :], rows[:, 0, :], vs[:, :], ALU.subtract))
                st.last()
                st.add(v.tensor_copy(dq[:, 0:1], tmp[:, 0:1]))
                st.add(v.tensor_tensor(dq[:, 1:TP], tmp[:, 1:TP], tmp[:, 0:TP - 1], ALU.subtract))
                st.last()
                for k in range(TG):
                    s = viota[:, k:k + 1]
                    st.add(v.tensor_scalar(tmp[:, :], vs[:, :], s, None, ALU.is_le, ALU.add,
                                           accum_out=tv[:, k:k + 1]))
                    st.add(v.scalar_tensor_tensor(rows[:, 0, :], vs[:, :], s, dq[:, :], ALU.is_le, ALU.mult,
                                                  accum_out=bv[:, k:k + 1]))
                    st.last()
                st.add(v.tensor_scalar(tv[:, :], tv[:, :], -1.0, None, ALU.add))
                st.add(v.tensor_tensor(bv[:, :], bv[:, :], viota[:, :], ALU.add))
                st.last()
                v.tensor_copy(tvI[:, :], tv[:, :]).then_inc(tv_ready, 1)
                st.add(v.tensor_scalar(tmp[:, 0:TG], bv[:, :], float(NB - 1), None, ALU.min))
                st.last()
                v.tensor_copy(bvI[:, :], tmp[:, 0:TG]).then_inc(tv_ready, 1)
                st.add(v.tensor_scalar(bv[:, :], bv[:, :], float(P), None, ALU.mult))
                st.last()

                def onehots(h, at):
                    v.tensor_tensor(OL[:, h, :, :], lowE[:, at].unsqueeze(2).to_broadcast([P, GV, P]),
                                    io_l[:, :].unsqueeze(1).to_broadcast([P, GV, P]), ALU.is_equal)
                    v.tensor_tensor(OB[:, h, :, :], blkD[:, at].unsqueeze(2).to_broadcast([P, GV, NB]),
                                    io_b[:, :].unsqueeze(1).to_broadcast([P, GV, NB]),
                                    ALU.is_equal).then_inc(oh_ready, 1)

                for h in range(2):
                    onehots(h, slice(h * GV, (h + 1) * GV))
                with v.Fori(1, NT // GV // 2) as i:
                    for h in range(2):
                        hold(v, oh_used, i * 2 + h - 1, pace["dve"])
                        onehots(h, bass.ds(i * (2 * GV) + h * GV, GV))
                v.wait_ge(gathered, 32 * TG)
                st.add(v.tensor_copy(dstVf[:, :, :], dstV[:, :, :]))
                v.tensor_copy(srcVf[:, :, :], srcV[:, :, :]).then_inc(vf_ready, 1)
                st.last()
                for k in range(TG):
                    ins = v.tensor_scalar(dstVf[:, k, :], dstVf[:, k, :], bv[:, k:k + 1], None, ALU.subtract)
                ins.then_inc(vf_ready, 1)
                for n in range(2 * TG):
                    v.wait_ge(turned, 2 * TG + n + 1)
                    to = (rel if n < TG else idx)[:, (n % TG) * P:(n % TG + 1) * P]
                    v.tensor_copy(to, tp[n % 2][:, 0:P]).then_inc(copied, 1)

                v.wait_ge(x_in, 32)
                v.wait_ge(written, 16)
                layernorm(v, st, X, D, X, stats, sm, mean[:, :], rstd[:, :], root_in, root_out)
                v.wait_ge(oh_used, NT // GV + 1)
                v.tensor_scalar(sm[:, 0, :], hist[:, 0:NB], 1.0, None, ALU.add).then_inc(root_in, 1)
                v.wait_ge(root_out, 2)
                st.add(v.reciprocal(dinv[:, :], sm[:, 1, :]))
                st.last()
                with v.Fori(0, NB // TB) as i:
                    for k in range(TB):
                        ins = v.tensor_scalar(ACC[:, bass.ds(i * (TB * W) + k * W, D)], X[:, bass.ds(i * (TB * D) + k * D, D)],
                                              dinv[:, bass.ds(i * TB + k, 1)], None, ALU.mult)
                    st.loop(i, 1)
                    st.add(ins)
                st.end(NB // TB)
                st.last()
                v.sem_inc(y_ready, 1)

        def aggregate(tag, table, weighted):
            with ExitStack() as sc:
                sb, pb, sem = mk(sc)
                G = sb(tag + "G", [P, SLOTS, GV, W])
                ring = sb(tag + "ring", [P, SLOTS, GV], I32)
                S = sb(tag + "S", [P, 2, GV, P])
                ps = [pb(f"{tag}ps{k}", [P, 512]) for k in range(GV)]
                idx_ready = sem(tag + "idx_ready")
                landed = [sem(f"{tag}landed{k}") for k in range(SLOTS)]
                onehot = sem(tag + "onehot")
                summed = sem(tag + "summed")
                added = sem(tag + "added")
                extra = sem(tag + "extra")
                block = sc.enter_context(nc.Block())

                @block.scalar
                def _(a):
                    a.wait_ge(extra, 1)

                    def fill(s, at):
                        if weighted:
                            a.copy(G[:, s, :, D + 1], ME[:, at])
                        a.copy(ring[:, s, :], idx[:, at]).then_inc(idx_ready, 1)

                    for s in range(SLOTS):
                        fill(s, slice(s * GV, (s + 1) * GV))
                    with a.Fori(1, NG // SLOTS) as g:
                        for s in range(SLOTS):
                            hold(a, summed, g * (SLOTS * GV) + (s - (SLOTS - 1)) * GV, pace["act"])
                            fill(s, bass.ds(g * (SLOTS * GV) + s * GV, GV))

                @block.gpsimd
                def _(p):
                    with p.Fori(0, NG // SLOTS) as g:
                        for s in range(SLOTS):
                            hold(p, idx_ready, g * SLOTS + s + 1, pace["pool"])
                            for k in range(GV):
                                p.indirect_dma_start(G[:, s, k, 0:D], None, table[:, :],
                                                     bass.IndirectOffsetOnAxis(ap=ring[:, s, k:k + 1], axis=0)
                                                     ).then_inc(landed[s], 16)

                @block.tensor
                def _(t):
                    with t.Fori(0, NG // SLOTS) as g:
                        for s in range(SLOTS):
                            t.wait_ge(landed[s], g * (16 * GV) + 16 * GV)
                            t.wait_ge(onehot, g * SLOTS + s + 1)
                            for k in range(GV):
                                if k % 4 == 0:
                                    t.wait_ge(added, g * (SLOTS * GV) + s * GV + k + 4)
                                t.matmul(ps[k][:, 0:W], S[:, s % 2, k, :], G[:, s, k, :], start=True, stop=True
                                         ).then_inc(summed, 1)

                @block.vector
                def _(v):
                    v.memset(G[:, :, :, D:W], 1.0).then_inc(extra, 1)
                    for k in range(GV):
                        v.sem_inc(added, 1)

                    def onehots(s, at):
                        for k in range(GV):
                            if weighted:
                                ins = v.tensor_scalar(S[:, s % 2, k, :], iota_f[:, :], rel[:, at(k)], WE[:, at(k)],
                                                      ALU.is_equal, ALU.mult)
                            else:
                                ins = v.tensor_scalar(S[:, s % 2, k, :], iota_f[:, :], rel[:, at(k)], None,
                                                      ALU.is_equal)
                        ins.then_inc(onehot, 1)

                    onehots(0, lambda k: slice(k, k + 1))
                    regs = [v.alloc_register(name=f"{tag}block{k}") for k in range(GV)]
                    with v.Fori(0, NG // SLOTS) as g:
                        for s in range(SLOTS):
                            onehots(s + 1, lambda k: bass.ds(g * (SLOTS * GV) + (s + 1) * GV + k, 1))
                            v.load(regs, blkv[0:1, bass.ds(g * (SLOTS * GV) + s * GV, GV)])
                            for k in range(GV):
                                b = v.snap(regs[k], min_val=0, max_val=NB - 1)
                                o = ACC[:, bass.ds(b * W, W)]
                                v.wait_ge(added, g * (SLOTS * GV) + s * GV + k + GV)
                                v.wait_ge(summed, g * (SLOTS * GV) + s * GV + k + 1)
                                v.tensor_tensor(o, o, ps[k][:, 0:W], ALU.add).then_inc(added, 1)

        aggregate("b_", table1, False)

        def skewed(eng, stages, n=NB):
            lag = len(stages) - 1
            first = lag + lag % 2 + 2
            for step in range(first):
                for j, f in enumerate(stages):
                    if step >= j:
                        f(step - j, (step - j) % 2)
            with eng.Fori(first // 2, n // 2) as i:
                for h in range(2):
                    for j, f in enumerate(stages):
                        f(i * 2 + (h - j), (h - j) % 2)
            for step in range(n, n + lag):
                for j, f in enumerate(stages):
                    if step - j < n:
                        f(step - j, (step - j) % 2)

        def reuse(eng, sem, n, pace):
            if not isinstance(n, int) or n >= 2:
                hold(eng, sem, n - 1, pace)

        with ExitStack() as sc:
            sb, pb, sem = mk(sc)
            W1 = sb("W1", [P, 2, D])
            W2 = sb("W2", [P, 2, W])
            b1c = sb("b1c", [P, 2])
            att = sb("att", [P, 2, D])
            junk = sb("junk", [P, D])
            T0 = sb("c_T0", [P, 2, D])
            AT = sb("c_AT", [P, 2, 2, P])
            HT = sb("c_HT", [P, 2, 2, P])
            pt = [pb(f"c_pt{i}", [P, 512]) for i in range(2)]
            ph = [pb(f"c_ph{i}", [P, 512]) for i in range(2)]
            px = [pb(f"c_px{i}", [P, 512]) for i in range(2)]
            w_in = sem("c_w_in")
            w_ready = sem("c_w_ready")
            scaled = sem("c_scaled")
            turned = sem("c_turned")
            at_ready = sem("c_at_ready")
            h_done = sem("c_h_done")
            h_ready = sem("c_h_ready")
            xw_done = sem("c_xw_done")
            xw_out = sem("c_xw_out")
            saved = sem("c_saved")
            block = sc.enter_context(nc.Block())

            @block.sync
            def _(sp):
                sp.dma_start(W1[:, :, :], gW1.rearrange("(k p) n -> p k n", p=P)).then_inc(w_in, 16)
                sp.dma_start(W2[:, :, 0:D], gW2.rearrange("(k p) n -> p k n", p=P)).then_inc(w_in, 16)
                sp.dma_start(att[:, 0, :], att_s.partition_broadcast(P)).then_inc(w_in, 16)
                sp.dma_start(att[:, 1, :], att_d.partition_broadcast(P)).then_inc(w_in, 16)
                sp.dma_start(b1c[:, :], gb1.rearrange("(k p) -> p k", p=P), allow_slow_non_contiguous=True).then_inc(w_in, 16)
                sp.wait_ge(xw_out, NB)
                sp.dma_start(node_rows(table2), Ab[:, :, 0:D]).then_inc(saved, 16)
                sp.wait_ge(saved, 16)

            @block.vector
            def _(v):
                v.wait_ge(w_in, 80)
                for j in range(2):
                    for k in range(2):
                        if j + k:
                            v.wait_ge(w_ready, 2 * j + k)
                        v.scalar_tensor_tensor(junk[:, :], W2[:, k, 0:D], 1.0, att[:, j, :], ALU.mult, ALU.mult,
                                               accum_out=W2[:, k, D + j:D + j + 1]).then_inc(w_ready, 1)

                def scale(n, par):
                    reuse(v, turned, n, pace["dve"])
                    v.tensor_scalar(T0[:, par, :], ACC[:, bass.ds(n * W, D)], dinv[:, bass.ds(n, 1)], None,
                                    ALU.mult).then_inc(scaled, 1)

                def keep(n, par):
                    hold(v, xw_done, n + 1, pace["dve"])
                    v.tensor_copy(ACC[:, bass.ds(n * W, D)], px[par][:, 0:D])
                    v.tensor_copy(AS[:, bass.ds(n, 1)], px[par][:, D:D + 1])
                    v.tensor_copy(AD[:, bass.ds(n, 1)], px[par][:, D + 1:D + 2]).then_inc(xw_out, 1)

                skewed(v, [scale, lambda n, par: None, keep])

            @block.scalar
            def _(a):
                a.wait_ge(w_in, 80)

                def turned_copy(n, par):
                    hold(a, turned, n + 1, pace["act"])
                    reuse(a, h_done, n, pace["act"])
                    a.copy(AT[:, par, :, :], pt[par][:, 0:D].rearrange("p (k q) -> p k q", k=2)).then_inc(at_ready, 1)

                def relu(n, par):
                    hold(a, h_done, n + 1, pace["act"])
                    reuse(a, xw_done, n, pace["act"])
                    for m in range(2):
                        ins = a.activation(HT[:, par, m, :], ph[par][:, m * P:(m + 1) * P], ACT.Relu,
                                           bias=b1c[:, m:m + 1])
                    ins.then_inc(h_ready, 1)

                skewed(a, [turned_copy, relu])

            @block.tensor
            def _(t):
                t.wait_ge(w_ready, 4)

                def turn(n, par):
                    hold(t, scaled, n + 1, pace["pe"])
                    reuse(t, at_ready, n, pace["pe"])
                    for k in range(2):
                        ins = t.transpose(pt[par][:, k * P:(k + 1) * P], T0[:, par, k * P:(k + 1) * P], ident[:, :])
                    ins.then_inc(turned, 1)

                def hidden(n, par):
                    hold(t, at_ready, n + 1, pace["pe"])
                    reuse(t, h_ready, n, pace["pe"])
                    for m in range(2):
                        for k in range(2):
                            ins = t.matmul(ph[par][:, m * P:(m + 1) * P], W1[:, k, m * P:(m + 1) * P],
                                           AT[:, par, k, :], start=(k == 0), stop=(k == 1))
                    ins.then_inc(h_done, 1)

                def xw(n, par):
                    hold(t, h_ready, n + 1, pace["pe"])
                    reuse(t, xw_out, n, pace["pe"])
                    for k in range(2):
                        ins = t.matmul(px[par][:, 0:W], HT[:, par, k, :], W2[:, k, :], start=(k == 0), stop=(k == 1))
                    ins.then_inc(xw_done, 1)

                skewed(t, [turn, hidden, xw])

        with ExitStack() as sc:
            sb, pb, sem = mk(sc)

            def spare(k):
                return ACC[:, k * TP:(k + 1) * TP].rearrange("p (g e) -> p g e", e=P)

            parts = sb("d_parts", [P, 2, 3, NB], BF16)
            rest = sb("d_rest", [P, 2, NB])
            LR = sb("d_LR", [P, 2, GV * P], BF16)
            LT = sb("d_LT", [P, 2, GV * P], BF16)
            OB = sb("d_OB", [P, 2, GV, NB], BF16)
            R = sb("d_R", [P, 2, GV, NB])
            pidx = sb("d_pidx", [P, 1])
            vals = sb("d_vals", [P, 2, TP])
            z = sb("d_z", [P, TP])
            Z = sb("d_Z", [P, TG, P])
            dI = sb("d_dI", [P, TG, P], I32)
            dF = spare(0)
            SF = spare(1)
            SB = spare(2)
            FW = spare(3)
            BW = spare(4)
            M = spare(5)
            e4 = sb("d_e4", [P, 4, TG])
            row = sb("d_row", [1, 4, TP])
            rw = sb("d_rw", [1, 6, TP])
            cr = sb("d_cr", [P, 2, TG])
            WV = ACC[:, 6 * TP:8 * TP].rearrange("p (j g e) -> p j g e", j=2, e=P)
            pr = [pb(f"d_pr{i}", [P, 512]) for i in range(2)]
            pt = [pb(f"d_pt{i}", [P, 512]) for i in range(2)]
            consts = sem("d_consts")
            parts_ready = sem("d_parts_ready")
            low_in = [sem("d_low_in0"), sem("d_low_in1")]
            lt_ready = sem("d_lt_ready")
            r_done = sem("d_r_done")
            picked = sem("d_picked")
            z_ready = sem("d_z_ready")
            turned = sem("d_turned")
            copied = sem("d_copied")
            d_in = sem("d_d_in")
            ends_ready = sem("d_ends_ready")
            moved = sem("d_moved")
            carry_ready = sem("d_carry_ready")
            e_ready = sem("d_e_ready")
            w_ready = sem("d_w_ready")
            wm_out = sem("d_wm_out")
            gathered = sem("d_gathered")
            steps = sem("d_steps")
            block = sc.enter_context(nc.Block())
            half = NT // GV

            @block.sync
            def _(sp):
                sp.dma_start(dI[:, :, :], dst_rows.rearrange("(g t) p -> t g p", t=P)).then_inc(d_in, 16)
                for j, low in enumerate((low_s, low_d)):
                    def load(i, h):
                        if not (isinstance(i, int) and j == 0):
                            hold(sp, lt_ready, i * 2 + h - 1 + j * half, pace["sp"])
                        sp.dma_start(LR[:, h, :], low[bass.ds(i * (2 * GV * P) + h * (GV * P), GV * P)
                                                      ].partition_broadcast(P)).then_inc(low_in[h], 16)
                    load(0, 0)
                    load(0, 1)
                    with sp.Fori(1, half // 2) as i:
                        load(i, 0)
                        load(i, 1)
                sp.wait_ge(ends_ready, 1)
                for k in range(4):
                    sp.dma_start(carry_rows[k, :].rearrange("(g t) -> t g", t=P), e4[:, k, :],
                                 allow_slow_non_contiguous=True).then_inc(moved, 16)
                sp.wait_ge(moved, 64)
                sp.dma_start(row[:, :, :], carry_rows.unsqueeze(0)).then_inc(moved, 16)
                sp.wait_ge(carry_ready, 1)
                for k in range(2):
                    sp.dma_start(carry_rows[k, :].unsqueeze(0), rw[:, k, :]).then_inc(moved, 16)
                sp.wait_ge(moved, 112)
                for k in range(2):
                    sp.dma_start(cr[:, k, :], carry_rows[k, :].rearrange("(g t) -> t g", t=P),
                                 allow_slow_non_contiguous=True).then_inc(moved, 16)
                sp.wait_ge(w_ready, 1)
                sp.dma_start(w_rows.rearrange("(g t) p -> t g p", t=P), Z[:, :, :]).then_inc(wm_out, 16)
                sp.dma_start(m_rows.rearrange("(g t) p -> t g p", t=P), M[:, :, :]).then_inc(wm_out, 16)
                sp.wait_ge(wm_out, 32)

            @block.gpsimd
            def _(g):
                g.iota(pidx[:, :], [[0, 1]], base=0, channel_multiplier=1,
                       allow_small_or_imprecise_dtypes=True).then_inc(consts, 1)
                g.wait_ge(wm_out, 32)
                for j, rows_d in enumerate((w_rows, m_rows)):
                    for k in range(TG):
                        g.indirect_dma_start(WV[:, j, k, :], None, rows_d[:, :],
                                             bass.IndirectOffsetOnAxis(ap=tvI[:, k:k + 1], axis=0)
                                             ).then_inc(gathered, 16)

            @block.scalar
            def _(a):
                a.wait_ge(e_ready, 1)
                a.activation(Z[:, :, :], Z[:, :, :], ACT.Exp).then_inc(w_ready, 1)

            @block.tensor
            def _(t):
                t.wait_ge(parts_ready, 1)
                for j in range(2):
                    def pick(i, h):
                        hold(t, lt_ready, i * 2 + h + 1 + j * half, pace["pe"])
                        if not (isinstance(i, int) and j == 0):
                            hold(t, picked, i * 2 + h - 1 + j * half, pace["pe"])
                        for k in range(GV):
                            for q in range(3):
                                ins = t.matmul(pr[h][:, k * NB:(k + 1) * NB], LT[:, h, k * P:(k + 1) * P],
                                               parts[:, j, q, :], start=(q == 0), stop=(q == 2))
                        ins.then_inc(r_done, 1)
                    pick(0, 0)
                    pick(0, 1)
                    with t.Fori(1, half // 2) as i:
                        pick(i, 0)
                        pick(i, 1)
                t.wait_ge(z_ready, 1)
                for k in range(TG):
                    if k >= 2:
                        t.wait_ge(copied, k - 1)
                    t.transpose(pt[k % 2][:, 0:P], z[:, k * P:(k + 1) * P], ident[:, :]).then_inc(turned, 1)
                t.wait_ge(gathered, 32 * TG)
                for n in range(2 * TG):
                    t.wait_ge(copied, TG + n - 1)
                    t.transpose(pt[(TG + n) % 2][:, 0:P], WV[:, n // TG, n % TG, :], ident[:, :]).then_inc(turned, 1)

            @block.vector
            def _(v):
                st = Steps(v, steps, pace["dve"])
                for j, A in enumerate((AS, AD)):
                    st.add(v.tensor_copy(parts[:, j, 0, :], A[:, :]))
                    st.last()
                    st.add(v.tensor_tensor(rest[:, j, :], A[:, :], parts[:, j, 0, :], ALU.subtract))
                    st.last()
                    st.add(v.tensor_copy(parts[:, j, 1, :], rest[:, j, :]))
                    st.last()
                    st.add(v.tensor_tensor(rest[:, j, :], rest[:, j, :], parts[:, j, 1, :], ALU.subtract))
                    st.last()
                    st.add(v.tensor_copy(parts[:, j, 2, :], rest[:, j, :]))
                st.add(v.memset(vals[:, :, :], 0.0))
                st.last()
                v.sem_inc(parts_ready, 1)
                v.wait_ge(consts, 1)
                for j in range(2):
                    blk = (blkS, blkD)[j]

                    def spread(i, h):
                        hold(v, low_in[h], i * 16 + 16 + j * (half // 2) * 16, pace["dve"])
                        if not (isinstance(i, int) and j == 0):
                            hold(v, r_done, i * 2 + h - 1 + j * half, pace["dve"])
                        v.tensor_scalar(LT[:, h, :], LR[:, h, :], pidx[:, :], None, ALU.is_equal)
                        v.tensor_tensor(OB[:, h, :, :],
                                        blk[:, bass.ds(i * (2 * GV) + h * GV, GV)].unsqueeze(2).to_broadcast([P, GV, NB]),
                                        io_b[:, :].unsqueeze(1).to_broadcast([P, GV, NB]),
                                        ALU.is_equal).then_inc(lt_ready, 1)

                    def pick(i, h):
                        hold(v, r_done, i * 2 + h + 1 + j * half, pace["dve"])
                        hold(v, lt_ready, i * 2 + h + 1 + j * half, pace["dve"])
                        v.tensor_tensor(R[:, h, :, :], pr[h][:, 0:GV * NB].rearrange("p (k b) -> p k b", b=NB),
                                        OB[:, h, :, :], ALU.mult).then_inc(picked, 1)
                        hold(v, picked, i * 2 + h + 1 + j * half, pace["dve"])
                        v.tensor_reduce(vals[:, j, bass.ds(i * (2 * GV) + h * GV, GV)], R[:, h, :, :], AX.X, ALU.add)

                    spread(0, 0)
                    with v.Fori(0, half // 2 - 1) as i:
                        spread(i, 1)
                        pick(i, 0)
                        spread(i + 1, 0)
                        pick(i, 1)
                    spread(half // 2 - 1, 1)
                    pick(half // 2 - 1, 0)
                    pick(half // 2 - 1, 1)
                st.add(v.memset(rw[:, 4, :], 0.0))
                st.last()
                st.add(v.tensor_tensor(z[:, :], vals[:, 0, :], vals[:, 1, :], ALU.add))
                st.last()
                v.scalar_tensor_tensor(z[:, :], z[:, :], SLOPE, z[:, :], ALU.mult, ALU.max).then_inc(z_ready, 1)
                for k in range(TG):
                    v.wait_ge(turned, k + 1)
                    v.tensor_copy(Z[:, k, :], pt[k % 2][:, 0:P]).then_inc(copied, 1)
                v.wait_ge(d_in, 16)
                st.add(v.tensor_copy(dF[:, :, :], dI[:, :, :]))
                st.last()
                st.add(v.memset(SF[:, :, :], -BIG))
                st.add(v.memset(SB[:, :, :], -BIG))
                st.add(v.tensor_tensor(FW[:, :, 1:P], dF[:, :, 1:P], dF[:, :, 0:P - 1], ALU.is_equal))
                st.last()
                st.add(v.tensor_scalar(SF[:, :, 1:P], FW[:, :, 1:P], -1.0, BIG, ALU.add, ALU.mult))
                st.add(v.tensor_scalar(SB[:, :, 0:P - 1], FW[:, :, 1:P], -1.0, BIG, ALU.add, ALU.mult))
                v.wait_ge(copied, TG)
                st.last()

                def flat(a):
                    return a[:, :, :].rearrange("p g e -> p (g e)")

                st.add(v.tensor_tensor_scan(flat(FW), flat(SF), flat(Z), -BIG, ALU.add, ALU.max))
                st.add(v.tensor_tensor_scan(flat(BW)[:, ::-1], flat(SB)[:, ::-1], flat(Z)[:, ::-1], -BIG,
                                            ALU.add, ALU.max))
                st.add(v.tensor_copy(e4[:, 0, :], dF[:, :, 0]))
                st.add(v.tensor_copy(e4[:, 1, :], dF[:, :, P - 1]))
                st.last()
                st.add(v.tensor_copy(e4[:, 2, :], FW[:, :, P - 1]))
                st.add(v.tensor_copy(e4[:, 3, :], BW[:, :, 0]))
                st.last()
                v.sem_inc(ends_ready, 1)
                v.wait_ge(moved, 80)
                first, last, fend, bend = (row[:, k, :] for k in range(4))
                one, cont, both, carry = rw[:, 2, :], rw[:, 3, :], rw[:, 5, :], rw[:, 4, :]
                st.add(v.memset(cont, -BIG))
                st.add(v.memset(carry, -BIG))
                st.add(v.memset(both, -BIG))
                st.add(v.memset(rw[:, 0:2, :], -BIG))
                st.add(v.tensor_tensor(one, first, last, ALU.is_equal))
                st.last()
                st.add(v.tensor_tensor(cont[:, 1:TP], first[:, 1:TP], last[:, 0:TP - 1], ALU.is_equal))
                st.last()
                st.add(v.tensor_scalar(cont[:, 1:TP], cont[:, 1:TP], -1.0, BIG, ALU.add, ALU.mult))
                st.add(v.tensor_scalar(one, one, -1.0, BIG, ALU.add, ALU.mult))
                st.last()
                st.add(v.tensor_tensor(both, cont, one, ALU.min))
                st.last()
                st.add(v.tensor_tensor_scan(carry, both, fend, -BIG, ALU.add, ALU.max))
                st.last()
                st.add(v.tensor_tensor(rw[:, 0, 1:TP], carry[:, 0:TP - 1], cont[:, 1:TP], ALU.add))
                st.last()
                st.add(v.memset(both[:, TP - 1:TP], -BIG))
                st.add(v.tensor_tensor(both[:, 0:TP - 1], cont[:, 1:TP], one[:, 0:TP - 1], ALU.min))
                st.last()
                st.add(v.tensor_tensor_scan(carry[:, ::-1], both[:, ::-1], bend[:, ::-1], -BIG, ALU.add, ALU.max))
                st.last()
                st.add(v.tensor_tensor(rw[:, 1, 0:TP - 1], carry[:, 1:TP], cont[:, 1:TP], ALU.add))
                st.last()
                v.sem_inc(carry_ready, 1)
                st.add(v.tensor_tensor(M[:, :, :], FW[:, :, :], BW[:, :, :], ALU.max))
                v.wait_ge(moved, 144)
                for k, end in ((0, 0), (1, P - 1)):
                    st.last()
                    st.add(v.tensor_tensor(SF[:, :, :], dF[:, :, :],
                                           dF[:, :, end:end + 1].to_broadcast([P, TG, P]), ALU.is_equal))
                    st.last()
                    st.add(v.tensor_scalar(SF[:, :, :], SF[:, :, :], -1.0, BIG, ALU.add, ALU.mult))
                    st.last()
                    st.add(v.tensor_tensor(SF[:, :, :], SF[:, :, :],
                                           cr[:, k, :].unsqueeze(2).to_broadcast([P, TG, P]), ALU.add))
                    st.last()
                    st.add(v.tensor_tensor(M[:, :, :], M[:, :, :], SF[:, :, :], ALU.max))
                st.last()
                v.tensor_tensor(Z[:, :, :], Z[:, :, :], M[:, :, :], ALU.subtract).then_inc(e_ready, 1)
                for n in range(2 * TG):
                    v.wait_ge(turned, TG + n + 1)
                    to = (WE if n < TG else ME)[:, (n % TG) * P:(n % TG + 1) * P]
                    v.tensor_copy(to, pt[(TG + n) % 2][:, 0:P]).then_inc(copied, 1)
                v.wait_ge(copied, 3 * TG)
                v.memset(ACC[:, :], 0.0)

        aggregate("e_", table2, True)

        edges.close()
        sb, pb, sem = mk(ctx)
        MX = sb("MX", [P, 2, D])
        wgt = sb("wgt", [P, 3, NB])

        with ExitStack() as sc:
            sb, pb, sem = mk(sc)
            KC = 2 * INNER // P
            WN = sb("m_WN", [P, 12, D])
            WO = sb("m_WO", [P, 2, INNER])
            WKV = sb("m_WKV", [P, 2, 2 * INNER])
            WOT = sb("m_WOT", [P, 4, D])
            hm = sb("m_hm", [P, 2, 2 * HEADS])
            zeros = sb("m_zeros", [P, INNER])
            T0 = sb("m_T0", [P, 2, D])
            XT = sb("m_XT", [P, 2, 2, P])
            SQ = sb("m_SQ", [P, 2, 2 * INNER])
            KS = sb("m_KS", [P, 2, INNER])
            VS = sb("m_VS", [P, 2, INNER])
            ss = sb("m_ss", [P, 2, 2 * HEADS])
            tt = sb("m_tt", [P, 2, 2 * HEADS])
            pp = sb("m_pp", [P, 2, HEADS])
            rt = sb("m_rt", [P, 2, HEADS])
            rr = sb("m_rr", [P, 2, HEADS])
            DOT = sb("m_DOT", [P, 4, P])
            TM = sb("m_TM", [P, 4, D])
            pt = [pb(f"m_pt{i}", [P, 512]) for i in range(2)]
            pk = [pb(f"m_pk{i}", [P, 1024]) for i in range(2)]
            pd = pb("m_pd", [P, 512])
            pe2 = pb("m_pe2", [P, 2, 256])
            w_in = sem("m_w_in")
            wt = sem("m_wt")
            wc = sem("m_wc")
            centred = sem("m_centred")
            taken = sem("m_taken")
            turned = sem("m_turned")
            xt_ready = sem("m_xt_ready")
            kv_done = sem("m_kv_done")
            sq_ready = sem("m_sq_ready")
            v_ready = sem("m_v_ready")
            stat = sem("m_stat")
            rooted = sem("m_rooted")
            k_ready = sem("m_k_ready")
            rec = sem("m_rec")
            dot_done = sem("m_dot_done")
            blk_ready = sem("m_blk_ready")
            tm_done = sem("m_tm_done")
            tm_ready = sem("m_tm_ready")
            mx_done = sem("m_mx_done")
            steps = sem("m_steps")
            block = sc.enter_context(nc.Block())
            turns = [(WN, 4 + c, f, WKV, f, c) for c in range(KC) for f in range(2)] + \
                    [(WO, o, j, WOT, j, o) for o in range(2) for j in range(4)]

            @block.sync
            def _(sp):
                sp.dma_start(WN[:, :, :], w_qkv.rearrange("(c p) d -> p c d", p=P)).then_inc(w_in, 16)
                sp.dma_start(WO[:, :, :], w_out.rearrange("(c p) d -> p c d", p=P)).then_inc(w_in, 16)

            @block.tensor
            def _(t):
                t.wait_ge(w_in, 32)
                for n, (a, c, f, _, _, _) in enumerate(turns):
                    if n >= 2:
                        t.wait_ge(wc, n - 1)
                    t.transpose(pk[n % 2][:, 0:P], a[:, c, f * P:(f + 1) * P], ident[:, :]).then_inc(wt, 1)
                t.wait_ge(centred, 1)

                def turn(n, par):
                    hold(t, taken, n + 1, pace["pe"])
                    reuse(t, xt_ready, n, pace["pe"])
                    for k in range(2):
                        ins = t.transpose(pt[par][:, k * P:(k + 1) * P], T0[:, par, k * P:(k + 1) * P], ident[:, :])
                    ins.then_inc(turned, 1)

                def kv(n, par):
                    hold(t, xt_ready, n + 1, pace["pe"])
                    reuse(t, k_ready, n, pace["pe"])
                    reuse(t, v_ready, n, pace["pe"])
                    for c in range(2):
                        for k in range(2):
                            ins = t.matmul(pk[par][:, c * INNER:(c + 1) * INNER], XT[:, par, k, :],
                                           WKV[:, k, c * INNER:(c + 1) * INNER], start=(k == 0), stop=(k == 1))
                    ins.then_inc(kv_done, 1)

                def dots(n, par):
                    hold(t, k_ready, n + 1, pace["pe"])
                    hold(t, v_ready, n + 1, pace["pe"])
                    for j in range(4):
                        ins = t.matmul(pd[:, j * P:(j + 1) * P], KS[:, par, j * P:(j + 1) * P],
                                       VS[:, par, j * P:(j + 1) * P], start=False, stop=False)
                    ins.then_inc(dot_done, 1)

                t.matmul(pd[:, :], zeros[:, 0:P], zeros[:, :], start=True, stop=False)
                skewed(t, [turn, kv, lambda n, par: None, dots])
                t.matmul(pd[:, :], zeros[:, 0:P], zeros[:, :], start=False, stop=True).then_inc(dot_done, 1)
                t.wait_ge(blk_ready, 1)
                for j in range(4):
                    ins = t.matmul(pk[j // 2][:, (j % 2) * D:(j % 2 + 1) * D], DOT[:, j, :], WN[:, j, :],
                                   start=True, stop=True)
                ins.then_inc(tm_done, 1)
                t.wait_ge(tm_ready, 2)
                for m in range(2):
                    for j in range(4):
                        ins = t.matmul(pe2[:, m, :], TM[:, j, m * P:(m + 1) * P], WOT[:, j, :],
                                       start=(j == 0), stop=(j == 3))
                ins.then_inc(mx_done, 1)

            @block.scalar
            def _(a):
                def take(n, par):
                    reuse(a, turned, n, pace["act"])
                    a.copy(T0[:, par, :], X[:, bass.ds(n * D, D)]).then_inc(taken, 1)

                def xt(n, par):
                    hold(a, turned, n + 1, pace["act"])
                    reuse(a, kv_done, n, pace["act"])
                    a.copy(XT[:, par, :, :], pt[par][:, 0:D].rearrange("p (k q) -> p k q", k=2)).then_inc(xt_ready, 1)

                def squares(n, par):
                    hold(a, kv_done, n + 1, pace["act"])
                    if not isinstance(n, int) or n >= 2:
                        hold(a, stat, n * 3 - 5, pace["act"])
                    a.activation(SQ[:, par, :], pk[par][:, :], ACT.Square).then_inc(sq_ready, 1)
                    reuse(a, dot_done, n, pace["act"])
                    a.copy(VS[:, par, :], pk[par][:, INNER:2 * INNER]).then_inc(v_ready, 1)

                def root(n, par):
                    hold(a, stat, n * 3 + 3, pace["act"])
                    reuse(a, k_ready, n, pace["act"])
                    a.activation(rt[:, par, :], pp[:, par, :], ACT.Sqrt).then_inc(rooted, 1)

                skewed(a, [take, xt, squares, root])

            @block.vector
            def _(v):
                st = Steps(v, steps, pace["dve"])
                for n, (_, _, _, to, c, f) in enumerate(turns):
                    v.wait_ge(wt, n + 1)
                    v.tensor_copy(to[:, c, f * P:(f + 1) * P], pk[n % 2][:, 0:P]).then_inc(wc, 1)
                v.wait_ge(wc, len(turns))
                st.add(v.memset(DOT[:, :, :], 0.0))
                st.add(v.memset(zeros[:, :], 0.0))
                for f in range(2):
                    w = WKV[:, f, :].rearrange("p (h e) -> p h e", e=DH)
                    st.add(v.tensor_reduce(hm[:, f, :], w, AX.X, ALU.add))
                    st.last()
                    st.add(v.tensor_scalar(hm[:, f, :], hm[:, f, :], 1.0 / DH, None, ALU.mult))
                    st.last()
                    st.add(v.tensor_tensor(w, w, hm[:, f, :].unsqueeze(2).to_broadcast([P, 2 * HEADS, DH]), ALU.subtract))
                st.last()
                v.sem_inc(centred, 1)

                def variances(n, par):
                    hold(v, sq_ready, n + 1, pace["dve"])
                    v.tensor_reduce(ss[:, par, :], SQ[:, par, :].rearrange("p (h e) -> p h e", e=DH), AX.X,
                                    ALU.add).then_inc(stat, 1)
                    hold(v, stat, n * 3 + 1, pace["dve"])
                    v.tensor_scalar(tt[:, par, :], ss[:, par, :], 1.0 / DH, EPS, ALU.mult, ALU.add).then_inc(stat, 1)
                    hold(v, stat, n * 3 + 2, pace["dve"])
                    reuse(v, rooted, n, pace["dve"])
                    v.tensor_tensor(pp[:, par, :], tt[:, par, 0:HEADS], tt[:, par, HEADS:], ALU.mult).then_inc(stat, 1)

                def scale(n, par):
                    hold(v, rooted, n + 1, pace["dve"])
                    v.reciprocal(rr[:, par, :], rt[:, par, :]).then_inc(rec, 1)
                    hold(v, rec, n + 1, pace["dve"])
                    reuse(v, dot_done, n, pace["dve"])
                    v.tensor_tensor(KS[:, par, :].rearrange("p (h e) -> p h e", e=DH),
                                    pk[par][:, 0:INNER].rearrange("p (h e) -> p h e", e=DH),
                                    rr[:, par, :].unsqueeze(2).to_broadcast([P, HEADS, DH]), ALU.mult
                                    ).then_inc(k_ready, 1)

                skewed(v, [lambda n, par: None, lambda n, par: None, variances, scale])
                v.wait_ge(dot_done, NB + 1)
                for h in range(2):
                    q = slice(h * DH, (h + 1) * DH)
                    ins = v.tensor_scalar(DOT[q, :, q], pd[q, :].rearrange("p (j e) -> p j e", e=P)[:, :, q],
                                          1.0 / N, None, ALU.mult)
                ins.then_inc(blk_ready, 1)
                v.wait_ge(tm_done, 1)
                for j in range(2):
                    v.tensor_copy(TM[:, 2 * j:2 * j + 2, :], pk[j][:, 0:2 * D].rearrange("p (j d) -> p j d", d=D)
                                  ).then_inc(tm_ready, 1)
                v.wait_ge(mx_done, 1)
                v.tensor_copy(MX[:, :, :], pe2[:, :, :])

        with ExitStack() as sc:
            sb, pb, sem = mk(sc)
            s1 = sb("f_s1", [P, 10, NB])
            brow = sb("f_brow", [P, 2, D])
            T0 = sb("f_T0", [P, 2, D])
            XT = sb("f_XT", [P, 2, 2, P])
            XW = sb("f_XW", [P, 2, D])
            XR = sb("f_XR", [P, 2, D])
            U = sb("f_U", [P, 2, D])
            stats = sb("f_stats", [P, NB * 6])
            sm = sb("f_sm", [P, 2, NB])
            mean = sb("f_mean", [P, NB])
            rstd = sb("f_rstd", [P, NB])
            pt = [pb(f"f_pt{i}", [P, 512]) for i in range(2)]
            pm = [pb(f"f_pm{i}", [P, 512]) for i in range(2)]
            w_in = sem("f_w_in")
            exps = sem("f_exps")
            exped = sem("f_exped")
            rows_in = [sem("f_rows_in0"), sem("f_rows_in1")]
            taken = sem("f_taken")
            turned = sem("f_turned")
            xt_ready = sem("f_xt_ready")
            mixed = sem("f_mixed")
            summed = sem("f_summed")
            root_in = sem("f_root_in")
            root_out = sem("f_root_out")
            steps = sem("f_steps")
            fs = sem("f_fs")
            block = sc.enter_context(nc.Block())

            @block.sync
            def _(sp):
                sp.dma_start(brow[:, 0, :], gb2.partition_broadcast(P)).then_inc(w_in, 16)
                sp.dma_start(brow[:, 1, :], b_out.partition_broadcast(P)).then_inc(w_in, 16)

                def load(n, par):
                    if not isinstance(n, int) or n >= 2:
                        hold(sp, summed, n - 1, pace["sp"])
                    sp.dma_start(XW[:, par, :], table2[bass.ds(n * P, P), :]).then_inc(rows_in[par], 16)
                    sp.dma_start(XR[:, par, :], x_pad[bass.ds(n * P, P), :]).then_inc(rows_in[par], 16)

                skewed(sp, [load])

            @block.scalar
            def _(a):
                a.wait_ge(exps, 1)
                a.activation(s1[:, 4:6, :], s1[:, 2:4, :], ACT.Exp).then_inc(exped, 1)

                def take(n, par):
                    reuse(a, turned, n, pace["act"])
                    a.copy(T0[:, par, :], X[:, bass.ds(n * D, D)]).then_inc(taken, 1)

                def xt(n, par):
                    hold(a, turned, n + 1, pace["act"])
                    reuse(a, mixed, n, pace["act"])
                    a.copy(XT[:, par, :, :], pt[par][:, 0:D].rearrange("p (k q) -> p k q", k=2)).then_inc(xt_ready, 1)

                skewed(a, [take, xt])
                a.wait_ge(root_in, 1)
                a.activation(sm[:, 1, :], sm[:, 0, :], ACT.Sqrt).then_inc(root_out, 1)

            @block.tensor
            def _(t):
                def turn(n, par):
                    hold(t, taken, n + 1, pace["pe"])
                    reuse(t, xt_ready, n, pace["pe"])
                    for k in range(2):
                        ins = t.transpose(pt[par][:, k * P:(k + 1) * P], T0[:, par, k * P:(k + 1) * P], ident[:, :])
                    ins.then_inc(turned, 1)

                def mix(n, par):
                    hold(t, xt_ready, n + 1, pace["pe"])
                    reuse(t, summed, n, pace["pe"])
                    for k in range(2):
                        ins = t.matmul(pm[par][:, 0:D], XT[:, par, k, :], MX[:, k, :], start=(k == 0), stop=(k == 1))
                    ins.then_inc(mixed, 1)

                skewed(t, [turn, mix])

            @block.vector
            def _(v):
                st = Steps(v, steps, pace["dve"])
                ssum, qsum = Ab[:, :, D], Ab[:, :, D + 1]
                st.add(v.tensor_tensor(s1[:, 0, :], AS[:, :], AD[:, :], ALU.add))
                st.add(v.tensor_scalar(s1[:, 1, :], ssum, 0.5, None, ALU.is_lt))
                st.last()
                st.add(v.scalar_tensor_tensor(s1[:, 0, :], s1[:, 0, :], SLOPE, s1[:, 0, :], ALU.mult, ALU.max))
                st.add(v.tensor_tensor(s1[:, 2, :], ssum, s1[:, 1, :], ALU.add))
                st.last()
                st.add(v.reciprocal(s1[:, 3, :], s1[:, 2, :]))
                st.last()
                st.add(v.tensor_tensor(s1[:, 2, :], qsum, s1[:, 3, :], ALU.mult))
                st.last()
                st.add(v.scalar_tensor_tensor(s1[:, 2, :], s1[:, 1, :], -BIG, s1[:, 2, :], ALU.mult, ALU.add))
                st.last()
                st.add(v.tensor_tensor(s1[:, 6, :], s1[:, 2, :], s1[:, 0, :], ALU.max))
                st.last()
                st.add(v.tensor_tensor(s1[:, 2, :], s1[:, 2, :], s1[:, 6, :], ALU.subtract))
                st.add(v.tensor_tensor(s1[:, 3, :], s1[:, 0, :], s1[:, 6, :], ALU.subtract))
                st.last()
                v.sem_inc(exps, 1)
                v.wait_ge(exped, 1)
                st.add(v.tensor_tensor(s1[:, 7, :], s1[:, 4, :], ssum, ALU.mult))
                st.last()
                st.add(v.scalar_tensor_tensor(s1[:, 7, :], s1[:, 7, :], 1e-16, s1[:, 5, :], ALU.add, ALU.add))
                st.last()
                st.add(v.reciprocal(s1[:, 8, :], s1[:, 7, :]))
                st.last()
                st.add(v.tensor_tensor(wgt[:, 0, :], s1[:, 4, :], s1[:, 8, :], ALU.mult))
                st.add(v.tensor_tensor(wgt[:, 1, :], s1[:, 5, :], s1[:, 8, :], ALU.mult))
                st.last()
                v.wait_ge(w_in, 32)

                def total(n, par):
                    acc, u = ACC[:, bass.ds(n * W, D)], U[:, par, :]

                    def step(k, ins):
                        ins.then_inc(fs, 1)
                        hold(v, fs, n * 5 + k + 1, pace["dve"])

                    hold(v, rows_in[par], n * 16 + (32 if par == 0 else 16), pace["dve"])
                    step(0, v.tensor_scalar(u, acc, wgt[:, 0, bass.ds(n, 1)], None, ALU.mult))
                    step(1, v.scalar_tensor_tensor(u, XW[:, par, :], wgt[:, 1, bass.ds(n, 1)], u, ALU.mult, ALU.add))
                    step(2, v.tensor_tensor(u, u, brow[:, 0, :], ALU.add))
                    step(3, v.scalar_tensor_tensor(u, u, 0.0, XR[:, par, :], ALU.max, ALU.add))
                    hold(v, mixed, n + 1, pace["dve"])
                    step(4, v.tensor_tensor(u, u, pm[par][:, 0:D], ALU.add))
                    v.tensor_tensor(acc, u, brow[:, 1, :], ALU.add).then_inc(summed, 1)

                skewed(v, [lambda n, par: None, total])
                v.wait_ge(summed, NB)
                layernorm(v, st, ACC, W, X, stats, sm, mean[:, :], rstd[:, :], root_in, root_out)

        with ExitStack() as sc:
            sb, pb, sem = mk(sc)
            F1 = sb("g_F1", [P, 2, NE, HID])
            F2 = sb("g_F2", [P, NE, HC, D])
            B1 = sb("g_B1", [P, NE, HC])
            B2 = sb("g_B2", [NE, D])
            GW = sb("g_GW", [P, 2, NE])
            GB = sb("g_GB", [1, NE])
            ones = sb("g_ones", [1, P])
            T0 = sb("g_T0", [P, TB, D])
            XT = sb("g_XT", [P, 2, TT])
            HT = sb("g_HT", [P, 2, HC, TT])
            SC = sb("g_SC", [P, TB, NE])
            C1 = sb("g_C1", [P, TB, NE, NE])
            C2 = sb("g_C2", [P, TB, NE, NE])
            tri = sb("g_tri", [P, NE, NE])
            MK = sb("g_MK", [P, TB, NE])
            pt = pb("g_pt", [P, 512])
            pg = pb("g_pg", [P, 512])
            ph = [pb(f"g_ph{i}", [P, 2, 512]) for i in range(2)]
            py = [pb(f"g_py{i}", [P, 512]) for i in range(2)]
            w_in = sem("g_w_in")
            consts = sem("g_consts")
            taken = sem("g_taken")
            turned = sem("g_turned")
            xt_ready = sem("g_xt_ready")
            gated = sem("g_gated")
            mk_steps = sem("g_mk_steps")
            h_done = sem("g_h_done")
            h_ready = sem("g_h_ready")
            y_done = sem("g_y_done")
            y_added = sem("g_y_added")
            stored = sem("g_stored")
            block = sc.enter_context(nc.Block())
            PT = 2 * TB
            half = TT // 2
            NQ = NE * HC
            NY = NE * TB

            @block.sync
            def _(sp):
                for k in range(2):
                    sp.dma_start(F1[:, k, :, :], fW1[:, k * P:(k + 1) * P, :].rearrange("e p h -> p e h")
                                 ).then_inc(w_in, 16)
                sp.dma_start(F2[:, :, :, :].rearrange("p e c d -> p (e c) d"),
                             fW2.rearrange("e h d -> (e h) d").rearrange("(c p) d -> p c d", p=P)).then_inc(w_in, 16)
                sp.dma_start(GW[:, :, :], Wg.rearrange("(k p) e -> p k e", p=P)).then_inc(w_in, 16)
                sp.dma_start(GB[:, :], bg.unsqueeze(0)).then_inc(w_in, 16)
                sp.dma_start(B2[:, :], fb2).then_inc(w_in, 16)
                sp.dma_start(B1[:, :, :].rearrange("p e c -> p (e c)"),
                             fb1.rearrange("e h -> (e h)").rearrange("(c p) -> p c", p=P),
                             allow_slow_non_contiguous=True).then_inc(w_in, 16)
                with sp.Fori(0, NB // TB - 1) as i:
                    hold(sp, y_added, i * NY + NY + 2, pace["sp"])
                    sp.dma_start(out[bass.ds(i * TT, TT), :].rearrange("(b l) d -> l b d", l=P),
                                 ACC[:, bass.ds(i * (TB * W), TB * W)].rearrange("p (b c) -> p b c", c=W)[:, :, 0:D]
                                 ).then_inc(stored, 16)
                last = NB - TB
                sp.wait_ge(y_added, NB // TB * NY + 2)
                sp.dma_start(out[last * P:FULL * P, :].rearrange("(b l) d -> l b d", l=P),
                             Ab[:, last:FULL, 0:D]).then_inc(stored, 16)
                sp.dma_start(out[FULL * P:N, :], Ab[0:REST, FULL, 0:D]).then_inc(stored, 16)
                sp.wait_ge(stored, 16 * (NB // TB + 1))

            @block.gpsimd
            def _(g):
                g.memset(tri[:, :, :], 1.0).then_inc(consts, 1)
                g.memset(ones[:, :], 1.0).then_inc(consts, 1)
                g.wait_ge(consts, 1)
                g.affine_select(out=tri[:, :, :], in_=tri[:, :, :], compare_op=ALU.is_gt, fill=0.0,
                                base=0, pattern=[[-1, NE], [1, NE]], channel_multiplier=0).then_inc(consts, 1)

            @block.scalar
            def _(a):
                a.wait_ge(w_in, 112)
                with a.Fori(0, NB // TB) as i:
                    hold(a, turned, i * PT + PT, pace["act"])
                    a.copy(T0[:, :, :], X[:, bass.ds(i * (TB * D), TB * D)].rearrange("p (b d) -> p b d", d=D)
                           ).then_inc(taken, 1)
                    for e in range(NE):
                        for c in range(HC):
                            q = e * HC + c
                            a.wait_ge(h_done, i * NQ + q + 1)
                            if c == 0:
                                a.wait_ge(y_done, i * NY + TB * e + TB)
                            a.activation(HT[:, e % 2, c, :].rearrange("p (s n) -> p s n", s=2), ph[q % 2][:, :, 0:half],
                                         ACT.Gelu, bias=B1[:, e, c:c + 1]).then_inc(h_ready, 1)

            @block.tensor
            def _(t):
                t.sem_inc(turned, PT)
                t.sem_inc(y_done, 2 * TB)
                t.wait_ge(w_in, 112)
                t.wait_ge(consts, 3)
                with t.Fori(0, NB // TB) as i:
                    hold(t, taken, i + 1, pace["pe"])
                    for b in range(TB):
                        hold(t, xt_ready, i * TB + b + 1, pace["pe"])
                        for k in range(2):
                            t.transpose(pt[:, (b % 2) * D + k * P:(b % 2) * D + (k + 1) * P],
                                        T0[:, b, k * P:(k + 1) * P], ident[:, :]).then_inc(turned, 1)
                    hold(t, xt_ready, i * TB + TB + 1, pace["pe"])
                    for b in range(TB):
                        o = pg[:, b * NE:(b + 1) * NE]
                        t.matmul(o, ones[:, :], GB[:, :], start=True, stop=False)
                        for k in range(2):
                            ins = t.matmul(o, XT[:, k, b * P:(b + 1) * P], GW[:, k, :], start=False, stop=(k == 1))
                    ins.then_inc(gated, 1)

                    def hidden(e):
                        for c in range(HC):
                            q = e * HC + c
                            hold(t, h_ready, i * NQ + q + 1, pace["pe"])
                            for s in range(2):
                                for k in range(2):
                                    ins = t.matmul(ph[q % 2][:, s, 0:half], F1[:, k, e, c * P:(c + 1) * P],
                                                   XT[:, k, s * half:(s + 1) * half], start=(k == 0), stop=(k == 1))
                            ins.then_inc(h_done, 1)

                    def outputs(e):
                        hold(t, h_ready, i * NQ + (e + 1) * HC + 2, pace["pe"])
                        for b in range(TB):
                            r = e * TB + b
                            hold(t, y_added, i * NY + r + 1, pace["pe"])
                            t.matmul(py[r % 2][:, 0:D], ident[0:NE, e:e + 1].to_broadcast([NE, P]), B2[:, :],
                                     start=True, stop=False)
                            for c in range(HC):
                                ins = t.matmul(py[r % 2][:, 0:D], HT[:, e % 2, c, b * P:(b + 1) * P], F2[:, e, c, :],
                                               start=False, stop=(c == HC - 1))
                            ins.then_inc(y_done, 1)

                    hidden(0)
                    for e in range(1, NE):
                        hidden(e)
                        outputs(e - 1)
                    outputs(NE - 1)

            @block.vector
            def _(v):
                v.sem_inc(xt_ready, 1)
                v.sem_inc(h_ready, 2)
                v.sem_inc(y_added, 2)
                v.wait_ge(consts, 3)
                with v.Fori(0, NB // TB) as i:
                    for b in range(TB):
                        hold(v, turned, i * PT + PT + 2 * b + 2, pace["dve"])
                        v.tensor_copy(XT[:, :, b * P:(b + 1) * P],
                                      pt[:, (b % 2) * D:(b % 2 + 1) * D].rearrange("p (k q) -> p k q", k=2)
                                      ).then_inc(xt_ready, 1)
                    hold(v, gated, i + 1, pace["dve"])

                    def step(k, ins):
                        ins.then_inc(mk_steps, 1)
                        hold(v, mk_steps, i * 6 + k + 1, pace["dve"])

                    step(0, v.tensor_copy(SC[:, :, :], pg[:, 0:TB * NE].rearrange("p (b e) -> p b e", e=NE)))
                    for b in range(TB):
                        mine = SC[:, b, :].unsqueeze(1).to_broadcast([P, NE, NE])
                        other = SC[:, b, :].unsqueeze(2).to_broadcast([P, NE, NE])
                        v.tensor_tensor(C1[:, b, :, :], other, mine, ALU.is_gt)
                        ins = v.tensor_tensor(C2[:, b, :, :], other, mine, ALU.is_equal)
                    step(1, ins)
                    step(2, v.tensor_tensor(C2[:, :, :, :].rearrange("p b i j -> p b (i j)"),
                                            C2[:, :, :, :].rearrange("p b i j -> p b (i j)"),
                                            tri[:, :, :].rearrange("p i j -> p (i j)").unsqueeze(1).to_broadcast([P, TB, NE * NE]),
                                            ALU.mult))
                    step(3, v.tensor_tensor(C1[:, :, :, :], C1[:, :, :, :], C2[:, :, :, :], ALU.add))
                    step(4, v.tensor_reduce(MK[:, :, :], C1[:, :, :, :].rearrange("p b i j -> p b j i"), AX.X, ALU.add))
                    step(5, v.tensor_scalar(MK[:, :, :], MK[:, :, :], 1.5, None, ALU.is_lt))
                    for e in range(NE):
                        for b in range(TB):
                            r = e * TB + b
                            acc = ACC[:, bass.ds(i * (TB * W) + b * W, D)]
                            v.wait_ge(y_done, i * NY + 2 * TB + r + 1)
                            v.wait_ge(y_added, i * NY + r + 2)
                            v.scalar_tensor_tensor(acc, py[r % 2][:, 0:D], MK[:, b, e:e + 1], acc, ALU.mult,
                                                   ALU.add).then_inc(y_added, 1)

_INS = ['x', 'src', 'dst', 'L0_gnn_W1', 'L0_gnn_b1', 'L0_gnn_W2', 'L0_gnn_att_src', 'L0_gnn_att_dst', 'L0_gnn_b2',
        'L0_mix_w_qkv', 'L0_mix_w_out', 'L0_mix_b_out', 'L0_ffn_Wg', 'L0_ffn_bg', 'L0_ffn_W1', 'L0_ffn_b1',
        'L0_ffn_W2', 'L0_ffn_b2']


def kernel(**inputs):
    import numpy as np
    import concourse.bacc as bacc
    from concourse.bass_utils import run_bass_kernel_spmd as run

    nc = bacc.Bacc("TRN2", target_bir_lowering=False, num_devices=1)
    arrays, args = {}, []
    for name in _INS:
        a = np.ascontiguousarray(inputs[name])
        arrays["in_" + name] = a
        args.append(nc.dram_tensor("in_" + name, a.shape, mybir.dt.from_np(a.dtype), kind="ExternalInput").ap())
    o = nc.dram_tensor("out_0", (N, D), F32, kind="ExternalOutput").ap()
    program(nc, *args, o)
    r = run(nc, [arrays], core_ids=[0])
    return r.results[0]["out_0"]
```

```python
import concourse.bass as bass
from concourse import mybir
from contextlib import ExitStack

F32 = mybir.dt.float32
BF16 = mybir.dt.bfloat16
I32 = mybir.dt.int32
ALU = mybir.AluOpType
ACT = mybir.ActivationFunctionType
AX = mybir.AxisListType

P = 128
N, D, E = 6250, 256, 100000
NB = 50
NP = NB * P
FULL = N // P
REST = N - FULL * P
TG = 7
TP = TG * P
NT = 784
GV = 8
NV = 832
NG = NV // GV
SLOTS = 4
W = D + 2
HEADS, DH = 8, 64
INNER = HEADS * DH
NE, HID = 8, 512
HC = HID // P
EPS = 1e-5
SLOPE = 0.2
XP = W
NTL = 108
GB_STEP = 10
BIG = 1e30
TB = 5
TT = TB * P


class Steps:

    def __init__(self, eng, sem, pace):
        self.eng, self.sem, self.pace, self.n, self.base = eng, sem, pace, 0, 0

    def add(self, ins):
        ins.then_inc(self.sem, 1)
        self.n += 1

    def last(self, plain=False):
        if self.n or not isinstance(self.base, int):
            hold(self.eng, self.sem, self.base + self.n, self.pace, plain)

    def loop(self, done, per):
        self.outer = (self.base, self.n, per)
        self.base, self.n = self.base + self.n + done * per, 0

    def end(self, bodies):
        base, n, per = self.outer
        assert self.n == per, (self.n, per)
        self.base, self.n = base, n + bodies * per


def hold(eng, sem, value, pace, plain=False):
    eng.wait_ge(sem, value)
    if not isinstance(value, int) and not plain:
        eng.sem_inc(pace, 1)


def layernorm(v, st, src, pitch, X, stats, sm, mean, rstd, act_root, root_done):
    st.last()
    with v.Fori(0, NB // TB) as i:
        for k in range(TB):
            ins = v.bn_stats(stats[:, bass.ds(i * (TB * 6) + k * 6, 6)],
                             src[:, bass.ds(i * (TB * pitch) + k * pitch, D)])
        st.loop(i, 1)
        st.add(ins)
    st.end(NB // TB)
    st.last()
    s = stats[:, :].rearrange("p (b s) -> p b s", s=6)
    m0, v0, m1, v1 = s[:, :, 1], s[:, :, 2], s[:, :, 4], s[:, :, 5]
    st.add(v.tensor_tensor(mean, m0, m1, ALU.add))
    st.add(v.tensor_tensor(rstd, m0, m1, ALU.subtract))
    st.last()
    st.add(v.tensor_scalar(mean, mean, 0.5, None, ALU.mult))
    st.add(v.scalar_tensor_tensor(sm[:, 0, :], rstd, 0.25, rstd, ALU.mult, ALU.mult))
    st.add(v.tensor_tensor(sm[:, 1, :], v0, v1, ALU.add))
    st.last()
    st.add(v.scalar_tensor_tensor(sm[:, 0, :], sm[:, 1, :], 1.0 / D, sm[:, 0, :], ALU.mult, ALU.add))
    st.last()
    v.tensor_scalar(sm[:, 0, :], sm[:, 0, :], EPS, None, ALU.add).then_inc(act_root, 1)
    v.wait_ge(root_done, 1)
    st.add(v.reciprocal(rstd, sm[:, 1, :]))
    st.last()
    with v.Fori(0, NB // TB) as i:
        for k in range(TB):
            ins = v.tensor_scalar(X[:, bass.ds(i * (TB * XP) + k * XP, D)],
                                  src[:, bass.ds(i * (TB * pitch) + k * pitch, D)], mean[:, bass.ds(i * TB + k, 1)], rstd[:, bass.ds(i * TB + k, 1)],
                                  ALU.subtract, ALU.mult)
        st.loop(i, 1)
        st.add(ins)
    st.end(NB // TB)
    st.last()


def node_rows(flat):
    return flat.rearrange("(b l) c -> l b c", l=P)


def program(nc, x, src, dst, gW1, gb1, gW2, att_s, att_d, gb2, w_qkv, w_out, b_out, Wg, bg, fW1, fb1, fW2, fb2, out):
    ctx = ExitStack()

    def dram(name, shape, dt=F32):
        return nc.dram_tensor(name, shape, dt, kind="Internal").ap()

    x_pad = dram("x_pad", (NP, D))
    table1 = dram("table1", (NP, D))
    table2 = dram("table2", (NP, D))
    src_rows = dram("src_rows", (TP, P), I32)
    dst_rows = dram("dst_rows", (TP, P), I32)
    ends = dram("ends", (4, TP))
    blk_row = dram("blk_row", (TP,), I32)
    low_s = dram("low_s", (TP * P,), BF16)
    low_d = dram("low_d", (TP * P,), BF16)
    w_rows = dram("w_rows", (TP, P))
    m_rows = dram("m_rows", (TP, P))
    carry_rows = dram("carry_rows", (4, TP))
    XS = dram("XS", (NTL * P, W))
    YS = dram("YS", ((2 * NP + NTL * P), D))

    with ctx:
        def mk(stack):
            return (lambda n, s, dt=F32: stack.enter_context(nc.sbuf_tensor(n, s, dt)),
                    lambda n, s, dt=F32: stack.enter_context(nc.psum_tensor(n, s, dt)),
                    lambda n: stack.enter_context(nc.semaphore(n)))

        sb, pb, sem = mk(ctx)
        X = sb("X", [P, NB * XP])
        ACC = sb("ACC", [P, NB * W])
        ident = sb("ident", [P, P])
        iota_f = sb("iota_f", [P, P])
        dinv = sb("dinv", [P, NB])
        AS = sb("AS", [P, NB])
        AD = sb("AD", [P, NB])
        eps_t = sb("eps_t", [P, 1])
        MX = sb("MX", [P, 2, D])
        pace = {n: sem("pace_" + n) for n in ("act", "pe", "dve", "pool", "sp")}
        Xb = X[:, :].rearrange("p (b d) -> p b d", d=XP)
        Ab = ACC[:, :].rearrange("p (b d) -> p b d", d=W)

        edges = ctx.enter_context(ExitStack())
        sb, pb, sem = mk(edges)
        idx = sb("idx", [P, TP], I32)
        rel = sb("rel", [P, TP])
        blkv = sb("blkv", [1, TP], I32)
        tvI = sb("tvI", [P, TG], I32)
        blkS = sb("blkS", [P, TP], BF16)
        blkD = sb("blkD", [P, TP], BF16)
        io_b = sb("io_b", [P, NB], BF16)

        with ExitStack() as sc:
            sb, pb, sem = mk(sc)
            stats = sb("stats", [P, NB * 6])
            sm = sb("sm", [P, 2, NB])
            mean = sb("mean", [P, NB])
            rstd = sb("rstd", [P, NB])
            sT = sb("sT", [P, TG, P], I32)
            dT = sb("dT", [P, TG, P], I32)
            dF = sb("dF", [P, TG, P])
            sF = sb("sF", [P, TG, P])
            sE = sb("sE", [P, TP], I32)
            lowI = sb("lowI", [P, TG, P], I32)
            lowsB = sb("lowsB", [P, TG, P], BF16)
            lowdB = sb("lowdB", [P, TG, P], BF16)
            endI = sb("endI", [P, 2, TG], I32)
            endF = sb("endF", [P, 4, TG])
            rows = sb("rows", [P, 2, TP])
            vs = sb("vs", [P, TP])
            dq = sb("dq", [P, TP])
            tmp = sb("tmp", [P, TP])
            tv = sb("tv", [P, TG])
            bv = sb("bv", [P, TG])
            bvI = sb("bvI", [P, TG], I32)
            viota = sb("viota", [P, TG])
            srcV = sb("srcV", [P, TG, P], I32)
            dstV = sb("dstV", [P, TG, P], I32)
            srcVf = sb("srcVf", [P, TG, P])
            dstVf = sb("dstVf", [P, TG, P])
            dE = sb("dE", [P, TP], I32)
            lowE = sb("lowE", [P, TP], BF16)
            blkEi = sb("blkEi", [P, TP], I32)
            io_l = sb("io_l", [P, P], BF16)
            OL = sb("OL", [P, 2, GV, P], BF16)
            OB = sb("OB", [P, 2, GV, NB], BF16)
            zero = sb("zero", [P, P], BF16)
            tp = [pb(f"tpA{i}", [P, 512]) for i in range(2)]
            hist = pb("hist", [P, 512])
            consts = sem("a_consts")
            padded = sem("a_padded")
            x_in = sem("a_x_in")
            e_in = sem("a_e_in")
            written = sem("a_written")
            tiles_out = sem("a_tiles_out")
            rows_in = sem("a_rows_in")
            ends_ready = sem("a_ends_ready")
            tv_ready = sem("a_tv_ready")
            bv_out = sem("a_bv_out")
            gathered = sem("a_gathered")
            vf_ready = sem("a_vf_ready")
            turned = sem("a_turned")
            copied = sem("a_copied")
            oh_ready = sem("a_oh_ready")
            oh_used = sem("a_oh_used")
            root_in = sem("a_root_in")
            root_out = sem("a_root_out")
            y_ready = sem("a_y_ready")
            steps = sem("a_steps")
            low_ready = sem("a_low_ready")
            block = sc.enter_context(nc.Block())

            @block.gpsimd
            def _(g):
                g.memset(ident[:, :], 0.0).then_inc(consts, 1)
                g.iota(iota_f[:, :], [[1, P]], base=0, channel_multiplier=0,
                       allow_small_or_imprecise_dtypes=True).then_inc(consts, 1)
                g.iota(viota[:, :], [[P, TG]], base=0, channel_multiplier=1,
                       allow_small_or_imprecise_dtypes=True).then_inc(consts, 1)
                g.memset(zero[:, :], 0.0).then_inc(consts, 1)
                g.wait_ge(consts, 4)
                g.affine_select(out=ident[:, :], in_=ident[:, :], compare_op=ALU.not_equal, fill=1.0,
                                base=0, pattern=[[-1, P]], channel_multiplier=1).then_inc(consts, 1)
                g.wait_ge(tiles_out, 32)
                g.wait_ge(tv_ready, 1)
                for k in range(TG):
                    for rows_d, to in ((src_rows, srcV), (dst_rows, dstV)):
                        g.indirect_dma_start(to[:, k, :], None, rows_d[:, :],
                                             bass.IndirectOffsetOnAxis(ap=tvI[:, k:k + 1], axis=0)
                                             ).then_inc(gathered, 16)

            @block.sync
            def _(sp):
                sp.wait_ge(padded, 4)
                body = slice(0, FULL * P)
                sp.dma_start(Xb[:, 0:FULL, 0:D], x[body, :].rearrange("(b l) d -> l b d", l=P)).then_inc(x_in, 16)
                sp.dma_start(Xb[0:REST, FULL, 0:D], x[FULL * P:N, :]).then_inc(x_in, 16)
                for a, to in ((src, sT), (dst, dT)):
                    whole = (TG - 1) * P * P
                    left = (E - whole) // P
                    sp.dma_start(to[:, 0:TG - 1, :], a[0:whole].rearrange("(g t p) -> t g p", p=P, t=P)).then_inc(e_in, 16)
                    sp.dma_start(to[0:left, TG - 1, :], a[whole:whole + left * P].rearrange("(t p) -> t p", p=P)).then_inc(e_in, 16)
                    sp.dma_start(to[left:left + 1, TG - 1, 0:E - whole - left * P],
                                 a[whole + left * P:E].unsqueeze(0)).then_inc(e_in, 16)
                sp.wait_ge(x_in, 32)
                sp.dma_start(node_rows(x_pad), Xb[:, :, 0:D]).then_inc(written, 16)
                sp.wait_ge(e_in, 96)
                sp.dma_start(src_rows.rearrange("(g t) p -> t g p", t=P), sT[:, :, :]).then_inc(tiles_out, 16)
                sp.dma_start(dst_rows.rearrange("(g t) p -> t g p", t=P), dT[:, :, :]).then_inc(tiles_out, 16)
                sp.wait_ge(ends_ready, 1)
                for k in range(4):
                    sp.dma_start(ends[k, :].rearrange("(g t) -> t g", t=P), endF[:, k, :], allow_slow_non_contiguous=True).then_inc(bv_out, 16)
                sp.wait_ge(bv_out, 64)
                for k in range(2):
                    sp.dma_start(rows[:, k, :], ends[k, :].partition_broadcast(P)).then_inc(rows_in, 16)
                sp.wait_ge(low_ready, 2)
                sp.dma_start(low_s.rearrange("(g t p) -> t g p", t=P, p=P), lowsB[:, :, :]).then_inc(written, 16)
                sp.dma_start(low_d.rearrange("(g t p) -> t g p", t=P, p=P), lowdB[:, :, :]).then_inc(written, 16)
                sp.wait_ge(tv_ready, 2)
                sp.dma_start(blk_row.rearrange("(g t) -> t g", t=P), bvI[:, :], allow_slow_non_contiguous=True).then_inc(bv_out, 16)
                sp.wait_ge(bv_out, 80)
                sp.dma_start(blkv[:, :], blk_row.unsqueeze(0)).then_inc(bv_out, 16)
                sp.wait_ge(y_ready, 1)
                sp.dma_start(node_rows(table1), Ab[:, :, 0:D]).then_inc(written, 16)
                sp.wait_ge(written, 64)
                sp.wait_ge(bv_out, 96)

            @block.scalar
            def _(a):
                a.wait_ge(root_in, 1)
                a.activation(sm[:, 1, :], sm[:, 0, :], ACT.Sqrt).then_inc(root_out, 1)
                a.wait_ge(root_in, 2)
                a.activation(sm[:, 1, :], sm[:, 0, :], ACT.Sqrt).then_inc(root_out, 1)

            @block.tensor
            def _(t):
                t.wait_ge(consts, 5)
                t.wait_ge(vf_ready, 1)
                for n in range(2 * TG):
                    if n >= 2:
                        t.wait_ge(copied, n - 1)
                    part = dF if n < TG else sF
                    t.transpose(tp[n % 2][:, 0:P], part[:, n % TG, :], ident[:, :]).then_inc(turned, 1)
                t.matmul(hist[:, 0:NB], zero[:, :], zero[:, 0:NB], start=True, stop=False)
                with t.Fori(0, NT // GV // 2) as i:
                    for h in range(2):
                        t.wait_ge(oh_ready, i * 2 + h + 1)
                        for k in range(GV):
                            mm = t.matmul(hist[:, 0:NB], OL[:, h, k, :], OB[:, h, k, :], start=False, stop=False)
                        mm.then_inc(oh_used, 1)
                t.matmul(hist[:, 0:NB], zero[:, :], zero[:, 0:NB], start=False, stop=True
                         ).then_inc(oh_used, 1)
                t.wait_ge(vf_ready, 3)
                for n in range(2 * TG):
                    part = dstVf if n < TG else srcVf
                    t.wait_ge(copied, 2 * TG + n - 1)
                    t.transpose(tp[n % 2][:, 0:P], part[:, n % TG, :], ident[:, :]).then_inc(turned, 1)

            @block.vector
            def _(v):
                st = Steps(v, steps, pace["dve"])
                v.memset(Xb[:, FULL:NB, :], 0.0).then_inc(padded, 1)
                v.memset(sT[:, TG - 1, :], 0).then_inc(padded, 1)
                v.memset(dT[:, TG - 1, :], NP - 1).then_inc(padded, 1)
                v.memset(eps_t[:, :], EPS).then_inc(padded, 1)
                st.add(v.memset(Ab[:, :, D:W], 0.0))
                v.wait_ge(e_in, 96)
                st.add(v.tensor_copy(dF[:, :, :], dT[:, :, :]))
                st.last()
                st.add(v.tensor_copy(endF[:, 2, :], dF[:, :, 0]))
                st.add(v.tensor_copy(sF[:, :, :], sT[:, :, :]))
                st.last()
                v.tensor_copy(endF[:, 3, :], dF[:, :, P - 1]).then_inc(vf_ready, 1)
                st.add(v.tensor_scalar(endI[:, 0, :], dT[:, :, 0], 7, None, ALU.arith_shift_right))
                st.add(v.tensor_scalar(endI[:, 1, :], dT[:, :, P - 1], 7, None, ALU.arith_shift_right))
                st.last()
                v.tensor_copy(endF[:, 0:2, :], endI[:, :, :]).then_inc(ends_ready, 1)
                st.add(v.tensor_scalar(lowI[:, :, :], sT[:, :, :], P - 1, None, ALU.bitwise_and))
                st.last()
                st.add(v.tensor_copy(lowsB[:, :, :], lowI[:, :, :]))
                st.last()
                v.sem_inc(low_ready, 1)
                st.add(v.tensor_scalar(lowI[:, :, :], dT[:, :, :], P - 1, None, ALU.bitwise_and))
                st.last()
                v.tensor_copy(lowdB[:, :, :], lowI[:, :, :]).then_inc(low_ready, 1)
                for n in range(2 * TG):
                    v.wait_ge(turned, n + 1)
                    to = (dE if n < TG else sE)[:, (n % TG) * P:(n % TG + 1) * P]
                    v.tensor_copy(to, tp[n % 2][:, 0:P]).then_inc(copied, 1)
                v.wait_ge(copied, 2 * TG)
                v.wait_ge(consts, 5)
                st.add(v.tensor_scalar(blkEi[:, :], dE[:, :], 7, None, ALU.arith_shift_right))
                st.add(v.tensor_scalar(dE[:, :], dE[:, :], P - 1, None, ALU.bitwise_and))
                st.add(v.tensor_copy(io_l[:, :], iota_f[:, :]))
                st.add(v.tensor_copy(io_b[:, :], iota_f[:, 0:NB]))
                st.last()
                st.add(v.tensor_copy(lowE[:, :], dE[:, :]))
                st.add(v.tensor_copy(blkD[:, :], blkEi[:, :]))
                st.add(v.tensor_scalar(sE[:, :], sE[:, :], 7, None, ALU.arith_shift_right))
                st.last()
                st.add(v.tensor_copy(blkS[:, :], sE[:, :]))

                v.wait_ge(rows_in, 32)
                st.add(v.tensor_tensor(tmp[:, :], rows[:, 1, :], rows[:, 0, :], ALU.subtract))
                st.last()
                st.add(v.tensor_scalar(tmp[:, :], tmp[:, :], 1.0, None, ALU.add))
                st.last()
                st.add(v.memset(dq[:, :], 0.0))
                st.last()
                st.add(v.tensor_tensor_scan(vs[:, :], tmp[:, :], dq[:, :], 0.0, ALU.add, ALU.add))
                st.last()
                st.add(v.tensor_tensor(vs[:, :], vs[:, :], tmp[:, :], ALU.subtract))
                st.last()
                st.add(v.tensor_tensor(tmp[:, :], rows[:, 0, :], vs[:, :], ALU.subtract))
                st.last()
                st.add(v.tensor_copy(dq[:, 0:1], tmp[:, 0:1]))
                st.add(v.tensor_tensor(dq[:, 1:TP], tmp[:, 1:TP], tmp[:, 0:TP - 1], ALU.subtract))
                st.last()
                for k in range(TG):
                    s = viota[:, k:k + 1]
                    st.add(v.tensor_scalar(tmp[:, :], vs[:, :], s, None, ALU.is_le, ALU.add,
                                           accum_out=tv[:, k:k + 1]))
                    st.add(v.scalar_tensor_tensor(rows[:, 0, :], vs[:, :], s, dq[:, :], ALU.is_le, ALU.mult,
                                                  accum_out=bv[:, k:k + 1]))
                    st.last()
                st.add(v.tensor_scalar(tv[:, :], tv[:, :], -1.0, None, ALU.add))
                st.add(v.tensor_tensor(bv[:, :], bv[:, :], viota[:, :], ALU.add))
                st.last()
                v.tensor_copy(tvI[:, :], tv[:, :]).then_inc(tv_ready, 1)
                st.add(v.tensor_scalar(tmp[:, 0:TG], bv[:, :], float(NB - 1), None, ALU.min))
                st.last()
                v.tensor_copy(bvI[:, :], tmp[:, 0:TG]).then_inc(tv_ready, 1)
                st.add(v.tensor_scalar(bv[:, :], bv[:, :], float(P), None, ALU.mult))
                st.last()

                def onehots(h, at):
                    v.tensor_tensor(OL[:, h, :, :], lowE[:, at].unsqueeze(2).to_broadcast([P, GV, P]),
                                    io_l[:, :].unsqueeze(1).to_broadcast([P, GV, P]), ALU.is_equal)
                    v.tensor_tensor(OB[:, h, :, :], blkD[:, at].unsqueeze(2).to_broadcast([P, GV, NB]),
                                    io_b[:, :].unsqueeze(1).to_broadcast([P, GV, NB]),
                                    ALU.is_equal).then_inc(oh_ready, 1)

                for h in range(2):
                    onehots(h, slice(h * GV, (h + 1) * GV))
                with v.Fori(1, NT // GV // 2) as i:
                    for h in range(2):
                        hold(v, oh_used, i * 2 + h - 1, pace["dve"])
                        onehots(h, bass.ds(i * (2 * GV) + h * GV, GV))
                v.wait_ge(gathered, 32 * TG)
                st.add(v.tensor_copy(dstVf[:, :, :], dstV[:, :, :]))
                v.tensor_copy(srcVf[:, :, :], srcV[:, :, :]).then_inc(vf_ready, 1)
                st.last()
                for k in range(TG):
                    ins = v.tensor_scalar(dstVf[:, k, :], dstVf[:, k, :], bv[:, k:k + 1], None, ALU.subtract)
                ins.then_inc(vf_ready, 1)
                for n in range(2 * TG):
                    v.wait_ge(turned, 2 * TG + n + 1)
                    to = (rel if n < TG else idx)[:, (n % TG) * P:(n % TG + 1) * P]
                    v.tensor_copy(to, tp[n % 2][:, 0:P]).then_inc(copied, 1)

                v.wait_ge(x_in, 32)
                v.wait_ge(written, 16)
                layernorm(v, st, X, XP, X, stats, sm, mean[:, :], rstd[:, :], root_in, root_out)
                v.wait_ge(oh_used, NT // GV + 1)
                v.tensor_scalar(sm[:, 0, :], hist[:, 0:NB], 1.0, None, ALU.add).then_inc(root_in, 1)
                v.wait_ge(root_out, 2)
                st.add(v.reciprocal(dinv[:, :], sm[:, 1, :]))
                st.last()
                with v.Fori(0, NB // TB) as i:
                    for k in range(TB):
                        ins = v.tensor_scalar(ACC[:, bass.ds(i * (TB * W) + k * W, D)], X[:, bass.ds(i * (TB * XP) + k * XP, D)],
                                              dinv[:, bass.ds(i * TB + k, 1)], None, ALU.mult)
                    st.loop(i, 1)
                    st.add(ins)
                st.end(NB // TB)
                st.last()
                v.sem_inc(y_ready, 1)

        def skewed(eng, stages, n=NB):
            lag = len(stages) - 1
            first = lag + lag % 2 + 2
            for step in range(first):
                for j, f in enumerate(stages):
                    if step >= j:
                        f(step - j, (step - j) % 2)
            with eng.Fori(first // 2, n // 2) as i:
                for h in range(2):
                    for j, f in enumerate(stages):
                        f(i * 2 + (h - j), (h - j) % 2)
            for step in range(n, n + lag):
                for j, f in enumerate(stages):
                    if step - j < n:
                        f(step - j, (step - j) % 2)

        def reuse(eng, sem, n, pace):
            if not isinstance(n, int) or n >= 2:
                hold(eng, sem, n - 1, pace)

        def aggregate(tag, table, weighted, side=None):
            turns = NG // SLOTS
            peeled = 3 if side else 0

            def rounds(eng, body, name):
                before, make, after = side[name] if side else (None, lambda eng: [], None)
                stages = make(eng)

                def steps_of(g):
                    def run(h):
                        for j, f in (reversed if name == "tensor" else iter)(list(enumerate(stages))):
                            m = g * 2 + (h - j)
                            if not isinstance(m, int) or 0 <= m < NB:
                                f(m, (h - j) % 2)
                    return run

                if before:
                    before(eng)
                if not side:
                    with eng.Fori(0, turns) as g:
                        body(g, steps_of(g))
                    return
                for g in range(peeled):
                    body(g, steps_of(g))
                last = NB // 2 - 1
                with eng.Fori(peeled, last) as g:
                    body(g, steps_of(g))
                for g in range(last, turns):
                    body(g, steps_of(g))
                for g in range(turns, (NB + len(stages)) // 2):
                    for h in range(2):
                        steps_of(g)(h)
                if after:
                    after(eng)

            with ExitStack() as sc:
                sb, pb, sem = mk(sc)
                banks = 4 if side else GV
                G = sb(tag + "G", [P, SLOTS, GV, W])
                ring = sb(tag + "ring", [P, SLOTS, GV], I32)
                S = sb(tag + "S", [P, 2, GV, P])
                ps = [pb(f"{tag}ps{k}", [P, 512]) for k in range(banks)]
                idx_ready = sem(tag + "idx_ready")
                landed = [sem(f"{tag}landed{k}") for k in range(SLOTS)]
                onehot = sem(tag + "onehot")
                summed = sem(tag + "summed")
                added = sem(tag + "added")
                extra = sem(tag + "extra")
                block = sc.enter_context(nc.Block())

                if side:
                    @block.sync
                    def _(sp):
                        side["sync"](sp)

                @block.scalar
                def _(a):
                    a.wait_ge(extra, 1)

                    def fill(s, at):
                        if weighted:
                            a.copy(G[:, s, :, D + 1], ME[:, at])
                        a.copy(ring[:, s, :], idx[:, at]).then_inc(idx_ready, 1)

                    for s in range(SLOTS):
                        fill(s, slice(s * GV, (s + 1) * GV))

                    def body(g, step):
                        for s in range(SLOTS):
                            if s % 2:
                                step(s // 2)
                            hold(a, summed, g * (SLOTS * GV) + (s + 1) * GV, pace["act"])
                            if not isinstance(g, int) or g < turns - 1:
                                fill(s, bass.ds(g * (SLOTS * GV) + (s + SLOTS) * GV, GV))

                    if side:
                        rounds(a, body, "scalar")
                    else:
                        with a.Fori(0, turns - 1) as g:
                            body(g, lambda h: None)

                @block.gpsimd
                def _(p):
                    with p.Fori(0, turns) as g:
                        for s in range(SLOTS):
                            hold(p, idx_ready, g * SLOTS + s + 1, pace["pool"])
                            for k in range(GV):
                                p.indirect_dma_start(G[:, s, k, 0:D], None, table[:, :],
                                                     bass.IndirectOffsetOnAxis(ap=ring[:, s, k:k + 1], axis=0)
                                                     ).then_inc(landed[s], 16)

                @block.tensor
                def _(t):
                    def body(g, step):
                        for s in range(SLOTS):
                            t.wait_ge(landed[s], g * (16 * GV) + 16 * GV)
                            t.wait_ge(onehot, g * SLOTS + s + 1)
                            every = 2 if banks == 4 else 4
                            for k in range(GV):
                                if k % every == 0:
                                    t.wait_ge(added, g * (SLOTS * GV) + s * GV + k + every)
                                t.matmul(ps[k % banks][:, 0:W], S[:, s % 2, k, :], G[:, s, k, :], start=True, stop=True
                                         ).then_inc(summed, 1)
                            if s % 2:
                                step(s // 2)

                    rounds(t, body, "tensor")

                @block.vector
                def _(v):
                    v.memset(G[:, :, :, D:W], 1.0).then_inc(extra, 1)
                    v.sem_inc(added, banks)

                    def onehots(s, at):
                        for k in range(GV):
                            if weighted:
                                ins = v.tensor_scalar(S[:, s % 2, k, :], iota_f[:, :], rel[:, at(k)], WE[:, at(k)],
                                                      ALU.is_equal, ALU.mult)
                            else:
                                ins = v.tensor_scalar(S[:, s % 2, k, :], iota_f[:, :], rel[:, at(k)], None,
                                                      ALU.is_equal)
                        ins.then_inc(onehot, 1)

                    onehots(0, lambda k: slice(k, k + 1))
                    regs = [v.alloc_register(name=f"{tag}block{k}") for k in range(GV)]

                    def body(g, step):
                        for s in range(SLOTS):
                            onehots(s + 1, lambda k: bass.ds(g * (SLOTS * GV) + (s + 1) * GV + k, 1))
                            v.load(regs, blkv[0:1, bass.ds(g * (SLOTS * GV) + s * GV, GV)])
                            for k in range(GV):
                                b = v.snap(regs[k], min_val=0, max_val=NB - 1)
                                o = ACC[:, bass.ds(b * W, W)]
                                v.wait_ge(added, g * (SLOTS * GV) + s * GV + k + banks)
                                v.wait_ge(summed, g * (SLOTS * GV) + s * GV + k + 1)
                                v.tensor_tensor(o, o, ps[k % banks][:, 0:W], ALU.add).then_inc(added, 1)
                            if s % 2:
                                step(s // 2)

                    rounds(v, body, "vector")

        def linear_attention(sc):
            sb, pb, sem = mk(sc)
            KC = 2 * INNER // P
            WQ = sb("m_WQ", [P, 4, D])
            WKV = sb("m_WKV", [P, 2, 2 * INNER])
            WOT = sb("m_WOT", [P, 4, D])
            hm = sb("m_hm", [P, 2, 2 * HEADS])
            zeros = sb("m_zeros", [P, INNER], BF16)
            T0 = sb("m_T0", [P, 2, D])
            XT = sb("m_XT", [P, 2, 2, P])
            SQ = sb("m_SQ", [P, 2, 2 * INNER])
            KR = sb("m_KR", [P, 2, INNER])
            KS = sb("m_KS", [P, 2, INNER])
            VS = sb("m_VS", [P, 2, INNER])
            ss = sb("m_ss", [P, 2, 2 * HEADS])
            tt = sb("m_tt", [P, 2, 2 * HEADS])
            pp = sb("m_pp", [P, 2, HEADS])
            rt = sb("m_rt", [P, 2, HEADS])
            rr = sb("m_rr", [P, 2, HEADS])
            DOT = sb("m_DOT", [P, 4, P])
            WN = SQ[:, :, :].rearrange("p a (c d) -> p (a c) d", d=D)
            WO = KS[:, :, :]
            TM = SQ[:, 0, :].rearrange("p (j d) -> p j d", d=D)
            pt = pb("m_pt", [P, 512])
            pk = pb("m_pk", [P, 1024])
            pd = pb("m_pd", [P, 512])
            w_in = sem("m_w_in")
            wt = sem("m_wt")
            wc = sem("m_wc")
            centred = sem("m_centred")
            taken = sem("m_taken")
            turned = sem("m_turned")
            xt_ready = sem("m_xt_ready")
            kv_done = sem("m_kv_done")
            sq_ready = sem("m_sq_ready")
            kv_ready = sem("m_kv_ready")
            stat = sem("m_stat")
            rooted = sem("m_rooted")
            k_ready = sem("m_k_ready")
            rec = sem("m_rec")
            dot_done = sem("m_dot_done")
            blk_ready = sem("m_blk_ready")
            tm_done = sem("m_tm_done")
            tm_ready = sem("m_tm_ready")
            mx_done = sem("m_mx_done")
            steps = sem("m_steps")
            turns = [(WN, c, f, WKV, f, c) for c in range(KC) for f in range(2)] + \
                    [(WO, o, j, WOT, j, o) for o in range(2) for j in range(4)]

            def load(sp):
                sp.dma_start(WN, w_qkv[INNER:, :].rearrange("(c p) d -> p c d", p=P)).then_inc(w_in, 16)
                sp.dma_start(WQ[:, :, :], w_qkv[0:INNER, :].rearrange("(c p) d -> p c d", p=P)).then_inc(w_in, 16)
                sp.dma_start(WO, w_out.rearrange("(c p) d -> p c d", p=P)).then_inc(w_in, 16)

            def pe_before(t):
                t.wait_ge(w_in, 48)
                for n, (a, c, f, _, _, _) in enumerate(turns):
                    if n >= 2:
                        t.wait_ge(wc, n - 1)
                    t.transpose(pk[:, (n % 2) * 512:(n % 2) * 512 + P], a[:, c, f * P:(f + 1) * P], ident[:, :]
                                ).then_inc(wt, 1)
                t.wait_ge(centred, 1)
                t.matmul(pd[:, :], zeros[:, 0:P], zeros[:, :], start=True, stop=False)

            def pe(t):
                def turn(n, par):
                    hold(t, taken, n + 1, pace["pe"])
                    if not isinstance(n, int) or n:
                        hold(t, xt_ready, n, pace["pe"])
                    for k in range(2):
                        ins = t.transpose(pt[:, k * P:(k + 1) * P], T0[:, par, k * P:(k + 1) * P], ident[:, :])
                    ins.then_inc(turned, 1)

                def kv(n, par):
                    hold(t, xt_ready, n + 1, pace["pe"])
                    if not isinstance(n, int) or n:
                        hold(t, kv_ready, n, pace["pe"])
                    for c in range(2):
                        for k in range(2):
                            ins = t.matmul(pk[:, c * INNER:(c + 1) * INNER], XT[:, par, k, :],
                                           WKV[:, k, c * INNER:(c + 1) * INNER], start=(k == 0), stop=(k == 1))
                    ins.then_inc(kv_done, 1)

                def dots(n, par):
                    hold(t, k_ready, n + 1, pace["pe"])
                    for j in range(4):
                        ins = t.matmul(pd[:, j * P:(j + 1) * P], KS[:, par, j * P:(j + 1) * P],
                                       VS[:, par, j * P:(j + 1) * P], start=False, stop=False)
                    ins.then_inc(dot_done, 1)

                return [turn, kv, lambda n, par: None, lambda n, par: None, dots]

            def pe_after(t):
                t.matmul(pd[:, :], zeros[:, 0:P], zeros[:, :], start=False, stop=True).then_inc(dot_done, 1)
                t.wait_ge(blk_ready, 1)
                for j in range(4):
                    ins = t.matmul(pk[:, j * D:(j + 1) * D], DOT[:, j, :], WQ[:, j, :], start=True, stop=True)
                ins.then_inc(tm_done, 1)
                t.wait_ge(tm_ready, 1)
                for m in range(2):
                    for j in range(4):
                        ins = t.matmul(pt[:, m * D:(m + 1) * D], TM[:, j, m * P:(m + 1) * P], WOT[:, j, :],
                                       start=(j == 0), stop=(j == 3))
                ins.then_inc(mx_done, 1)

            def act(a):
                def take(n, par):
                    reuse(a, turned, n, pace["act"])
                    a.copy(T0[:, par, :], X[:, bass.ds(n * XP, D)]).then_inc(taken, 1)

                def xt(n, par):
                    hold(a, turned, n + 1, pace["act"])
                    reuse(a, kv_done, n, pace["act"])
                    a.copy(XT[:, par, :, :], pt[:, 0:D].rearrange("p (k q) -> p k q", k=2)).then_inc(xt_ready, 1)

                def squares(n, par):
                    if isinstance(n, int) and n == 0:
                        a.wait_ge(centred, 1)
                    hold(a, kv_done, n + 1, pace["act"])
                    if not isinstance(n, int) or n >= 2:
                        hold(a, stat, n * 3 - 5, pace["act"])
                    a.activation(SQ[:, par, :], pk[:, :], ACT.Square).then_inc(sq_ready, 1)
                    reuse(a, dot_done, n, pace["act"])
                    a.copy(VS[:, par, :], pk[:, INNER:2 * INNER])
                    a.copy(KR[:, par, :], pk[:, 0:INNER]).then_inc(kv_ready, 1)

                def root(n, par):
                    hold(a, stat, n * 3 + 3, pace["act"])
                    reuse(a, k_ready, n, pace["act"])
                    a.activation(rt[:, par, :], pp[:, par, :], ACT.Sqrt).then_inc(rooted, 1)

                return [take, xt, squares, root]

            def dve_before(v):
                st = Steps(v, steps, pace["dve"])
                for n, (_, _, _, to, c, f) in enumerate(turns):
                    v.wait_ge(wt, n + 1)
                    v.tensor_copy(to[:, c, f * P:(f + 1) * P], pk[:, (n % 2) * 512:(n % 2) * 512 + P]).then_inc(wc, 1)
                v.wait_ge(wc, len(turns))
                st.add(v.memset(DOT[:, :, :], 0.0))
                st.add(v.memset(zeros[:, :], 0.0))
                for f in range(2):
                    w = WKV[:, f, :].rearrange("p (h e) -> p h e", e=DH)
                    st.add(v.tensor_reduce(hm[:, f, :], w, AX.X, ALU.add))
                    st.last()
                    st.add(v.tensor_scalar(hm[:, f, :], hm[:, f, :], 1.0 / DH, None, ALU.mult))
                    st.last()
                    st.add(v.tensor_tensor(w, w, hm[:, f, :].unsqueeze(2).to_broadcast([P, 2 * HEADS, DH]), ALU.subtract))
                st.last()
                v.sem_inc(centred, 1)

            def dve(v):
                def variances(n, par):
                    hold(v, sq_ready, n + 1, pace["dve"])
                    v.tensor_reduce(ss[:, par, :], SQ[:, par, :].rearrange("p (h e) -> p h e", e=DH), AX.X,
                                    ALU.add).then_inc(stat, 1)
                    hold(v, stat, n * 3 + 1, pace["dve"])
                    v.tensor_scalar(tt[:, par, :], ss[:, par, :], 1.0 / DH, EPS, ALU.mult, ALU.add).then_inc(stat, 1)
                    hold(v, stat, n * 3 + 2, pace["dve"])
                    reuse(v, rooted, n, pace["dve"])
                    v.tensor_tensor(pp[:, par, :], tt[:, par, 0:HEADS], tt[:, par, HEADS:], ALU.mult).then_inc(stat, 1)

                def scale(n, par):
                    hold(v, rooted, n + 1, pace["dve"])
                    v.reciprocal(rr[:, par, :], rt[:, par, :]).then_inc(rec, 1)
                    hold(v, rec, n + 1, pace["dve"])
                    hold(v, kv_ready, n + 1, pace["dve"])
                    reuse(v, dot_done, n, pace["dve"])
                    v.tensor_tensor(KS[:, par, :].rearrange("p (h e) -> p h e", e=DH),
                                    KR[:, par, :].rearrange("p (h e) -> p h e", e=DH),
                                    rr[:, par, :].unsqueeze(2).to_broadcast([P, HEADS, DH]), ALU.mult
                                    ).then_inc(k_ready, 1)

                return [lambda n, par: None, lambda n, par: None, variances, scale]

            def dve_after(v):
                v.wait_ge(dot_done, NB + 1)
                for h in range(2):
                    q = slice(h * DH, (h + 1) * DH)
                    ins = v.tensor_scalar(DOT[q, :, q], pd[q, :].rearrange("p (j e) -> p j e", e=P)[:, :, q],
                                          1.0 / N, None, ALU.mult)
                ins.then_inc(blk_ready, 1)
                v.wait_ge(tm_done, 1)
                v.tensor_copy(TM, pk[:, :].rearrange("p (j d) -> p j d", d=D)).then_inc(tm_ready, 1)
                v.wait_ge(mx_done, 1)
                v.tensor_copy(MX[:, :, :], pt[:, :].rearrange("p (m d) -> p m d", d=D))

            return {"sync": load, "tensor": (pe_before, pe, pe_after), "scalar": (None, act, None),
                    "vector": (dve_before, dve, dve_after)}

        with ExitStack() as sc:
            aggregate("b_", table1, False, linear_attention(sc))

        sb, pb, sem = mk(edges)
        WE = sb("WE", [P, TP])
        ME = sb("ME", [P, TP])

        with ExitStack() as sc:
            sb, pb, sem = mk(sc)
            W1 = sb("W1", [P, 2, D])
            W2 = sb("W2", [P, 2, W])
            b1c = sb("b1c", [P, 2])
            att = sb("att", [P, 2, D])
            junk = sb("junk", [P, D])
            T0 = sb("c_T0", [P, 2, D])
            AT = sb("c_AT", [P, 2, 2, P])
            HT = sb("c_HT", [P, 2, 2, P])
            pt = [pb(f"c_pt{i}", [P, 512]) for i in range(2)]
            ph = [pb(f"c_ph{i}", [P, 512]) for i in range(2)]
            px = [pb(f"c_px{i}", [P, 512]) for i in range(2)]
            w_in = sem("c_w_in")
            w_ready = sem("c_w_ready")
            scaled = sem("c_scaled")
            turned = sem("c_turned")
            at_ready = sem("c_at_ready")
            h_done = sem("c_h_done")
            h_ready = sem("c_h_ready")
            xw_done = sem("c_xw_done")
            xw_out = sem("c_xw_out")
            saved = sem("c_saved")
            block = sc.enter_context(nc.Block())

            @block.sync
            def _(sp):
                sp.dma_start(W1[:, :, :], gW1.rearrange("(k p) n -> p k n", p=P)).then_inc(w_in, 16)
                sp.dma_start(W2[:, :, 0:D], gW2.rearrange("(k p) n -> p k n", p=P)).then_inc(w_in, 16)
                sp.dma_start(att[:, 0, :], att_s.partition_broadcast(P)).then_inc(w_in, 16)
                sp.dma_start(att[:, 1, :], att_d.partition_broadcast(P)).then_inc(w_in, 16)
                sp.dma_start(b1c[:, :], gb1.rearrange("(k p) -> p k", p=P), allow_slow_non_contiguous=True).then_inc(w_in, 16)
                sp.wait_ge(xw_out, NB)
                sp.dma_start(node_rows(table2), Ab[:, :, 0:D]).then_inc(saved, 16)
                sp.wait_ge(saved, 16)

            @block.vector
            def _(v):
                v.wait_ge(w_in, 80)
                for j in range(2):
                    for k in range(2):
                        if j + k:
                            v.wait_ge(w_ready, 2 * j + k)
                        v.scalar_tensor_tensor(junk[:, :], W2[:, k, 0:D], 1.0, att[:, j, :], ALU.mult, ALU.mult,
                                               accum_out=W2[:, k, D + j:D + j + 1]).then_inc(w_ready, 1)

                def scale(n, par):
                    reuse(v, turned, n, pace["dve"])
                    v.tensor_scalar(T0[:, par, :], ACC[:, bass.ds(n * W, D)], dinv[:, bass.ds(n, 1)], None,
                                    ALU.mult).then_inc(scaled, 1)

                def keep(n, par):
                    hold(v, xw_done, n + 1, pace["dve"])
                    v.tensor_copy(ACC[:, bass.ds(n * W, D)], px[par][:, 0:D])
                    v.tensor_copy(AS[:, bass.ds(n, 1)], px[par][:, D:D + 1])
                    v.tensor_copy(AD[:, bass.ds(n, 1)], px[par][:, D + 1:D + 2]).then_inc(xw_out, 1)

                skewed(v, [scale, lambda n, par: None, keep])

            @block.scalar
            def _(a):
                a.wait_ge(w_in, 80)

                def turned_copy(n, par):
                    hold(a, turned, n + 1, pace["act"])
                    reuse(a, h_done, n, pace["act"])
                    a.copy(AT[:, par, :, :], pt[par][:, 0:D].rearrange("p (k q) -> p k q", k=2)).then_inc(at_ready, 1)

                def relu(n, par):
                    hold(a, h_done, n + 1, pace["act"])
                    reuse(a, xw_done, n, pace["act"])
                    for m in range(2):
                        ins = a.activation(HT[:, par, m, :], ph[par][:, m * P:(m + 1) * P], ACT.Relu,
                                           bias=b1c[:, m:m + 1])
                    ins.then_inc(h_ready, 1)

                skewed(a, [turned_copy, relu])

            @block.tensor
            def _(t):
                t.wait_ge(w_ready, 4)

                def turn(n, par):
                    hold(t, scaled, n + 1, pace["pe"])
                    reuse(t, at_ready, n, pace["pe"])
                    for k in range(2):
                        ins = t.transpose(pt[par][:, k * P:(k + 1) * P], T0[:, par, k * P:(k + 1) * P], ident[:, :])
                    ins.then_inc(turned, 1)

                def hidden(n, par):
                    hold(t, at_ready, n + 1, pace["pe"])
                    reuse(t, h_ready, n, pace["pe"])
                    for m in range(2):
                        for k in range(2):
                            ins = t.matmul(ph[par][:, m * P:(m + 1) * P], W1[:, k, m * P:(m + 1) * P],
                                           AT[:, par, k, :], start=(k == 0), stop=(k == 1))
                    ins.then_inc(h_done, 1)

                def xw(n, par):
                    hold(t, h_ready, n + 1, pace["pe"])
                    reuse(t, xw_out, n, pace["pe"])
                    for k in range(2):
                        ins = t.matmul(px[par][:, 0:W], HT[:, par, k, :], W2[:, k, :], start=(k == 0), stop=(k == 1))
                    ins.then_inc(xw_done, 1)

                skewed(t, [turn, hidden, xw])

        with ExitStack() as sc:
            sb, pb, sem = mk(sc)

            def spare(k):
                return ACC[:, k * TP:(k + 1) * TP].rearrange("p (g e) -> p g e", e=P)

            parts = sb("d_parts", [P, 2, 3, NB], BF16)
            rest = sb("d_rest", [P, 2, NB])
            LR = sb("d_LR", [P, 2, GV * P], BF16)
            LT = sb("d_LT", [P, 2, GV * P], BF16)
            OB = sb("d_OB", [P, 2, GV, NB], BF16)
            R = sb("d_R", [P, 2, GV, NB])
            pidx = sb("d_pidx", [P, 1])
            vals = sb("d_vals", [P, 2, TP])
            z = sb("d_z", [P, TP])
            Z = sb("d_Z", [P, TG, P])
            dI = sb("d_dI", [P, TG, P], I32)
            dF = spare(0)
            SF = spare(1)
            SB = spare(2)
            FW = spare(3)
            BW = spare(4)
            M = spare(5)
            e4 = sb("d_e4", [P, 4, TG])
            row = sb("d_row", [1, 4, TP])
            rw = sb("d_rw", [1, 6, TP])
            cr = sb("d_cr", [P, 2, TG])
            WV = ACC[:, 6 * TP:8 * TP].rearrange("p (j g e) -> p j g e", j=2, e=P)
            pr = [pb(f"d_pr{i}", [P, 512]) for i in range(2)]
            pt = [pb(f"d_pt{i}", [P, 512]) for i in range(2)]
            consts = sem("d_consts")
            parts_ready = sem("d_parts_ready")
            low_in = [sem("d_low_in0"), sem("d_low_in1")]
            lt_ready = sem("d_lt_ready")
            r_done = sem("d_r_done")
            picked = sem("d_picked")
            z_ready = sem("d_z_ready")
            turned = sem("d_turned")
            copied = sem("d_copied")
            d_in = sem("d_d_in")
            ends_ready = sem("d_ends_ready")
            moved = sem("d_moved")
            carry_ready = sem("d_carry_ready")
            e_ready = sem("d_e_ready")
            w_ready = sem("d_w_ready")
            wm_out = sem("d_wm_out")
            gathered = sem("d_gathered")
            steps = sem("d_steps")
            block = sc.enter_context(nc.Block())
            half = NT // GV

            @block.sync
            def _(sp):
                sp.dma_start(dI[:, :, :], dst_rows.rearrange("(g t) p -> t g p", t=P)).then_inc(d_in, 16)
                for j, low in enumerate((low_s, low_d)):
                    def load(i, h):
                        if not (isinstance(i, int) and j == 0):
                            hold(sp, lt_ready, i * 2 + h - 1 + j * half, pace["sp"])
                        sp.dma_start(LR[:, h, :], low[bass.ds(i * (2 * GV * P) + h * (GV * P), GV * P)
                                                      ].partition_broadcast(P)).then_inc(low_in[h], 16)
                    load(0, 0)
                    load(0, 1)
                    with sp.Fori(1, half // 2) as i:
                        load(i, 0)
                        load(i, 1)
                sp.wait_ge(ends_ready, 1)
                for k in range(4):
                    sp.dma_start(carry_rows[k, :].rearrange("(g t) -> t g", t=P), e4[:, k, :],
                                 allow_slow_non_contiguous=True).then_inc(moved, 16)
                sp.wait_ge(moved, 64)
                sp.dma_start(row[:, :, :], carry_rows.unsqueeze(0)).then_inc(moved, 16)
                sp.wait_ge(carry_ready, 1)
                for k in range(2):
                    sp.dma_start(carry_rows[k, :].unsqueeze(0), rw[:, k, :]).then_inc(moved, 16)
                sp.wait_ge(moved, 112)
                for k in range(2):
                    sp.dma_start(cr[:, k, :], carry_rows[k, :].rearrange("(g t) -> t g", t=P),
                                 allow_slow_non_contiguous=True).then_inc(moved, 16)
                sp.wait_ge(w_ready, 1)
                sp.dma_start(w_rows.rearrange("(g t) p -> t g p", t=P), Z[:, :, :]).then_inc(wm_out, 16)
                sp.dma_start(m_rows.rearrange("(g t) p -> t g p", t=P), M[:, :, :]).then_inc(wm_out, 16)
                sp.wait_ge(wm_out, 32)

            @block.gpsimd
            def _(g):
                g.iota(pidx[:, :], [[0, 1]], base=0, channel_multiplier=1,
                       allow_small_or_imprecise_dtypes=True).then_inc(consts, 1)
                g.wait_ge(wm_out, 32)
                for j, rows_d in enumerate((w_rows, m_rows)):
                    for k in range(TG):
                        g.indirect_dma_start(WV[:, j, k, :], None, rows_d[:, :],
                                             bass.IndirectOffsetOnAxis(ap=tvI[:, k:k + 1], axis=0)
                                             ).then_inc(gathered, 16)

            @block.scalar
            def _(a):
                a.wait_ge(e_ready, 1)
                a.activation(Z[:, :, :], Z[:, :, :], ACT.Exp).then_inc(w_ready, 1)

            @block.tensor
            def _(t):
                t.wait_ge(parts_ready, 1)
                for j in range(2):
                    def pick(i, h):
                        hold(t, lt_ready, i * 2 + h + 1 + j * half, pace["pe"])
                        if not (isinstance(i, int) and j == 0):
                            hold(t, picked, i * 2 + h - 1 + j * half, pace["pe"])
                        for k in range(GV):
                            for q in range(3):
                                ins = t.matmul(pr[h][:, k * NB:(k + 1) * NB], LT[:, h, k * P:(k + 1) * P],
                                               parts[:, j, q, :], start=(q == 0), stop=(q == 2))
                        ins.then_inc(r_done, 1)
                    pick(0, 0)
                    pick(0, 1)
                    with t.Fori(1, half // 2) as i:
                        pick(i, 0)
                        pick(i, 1)
                t.wait_ge(z_ready, 1)
                for k in range(TG):
                    if k >= 2:
                        t.wait_ge(copied, k - 1)
                    t.transpose(pt[k % 2][:, 0:P], z[:, k * P:(k + 1) * P], ident[:, :]).then_inc(turned, 1)
                t.wait_ge(gathered, 32 * TG)
                for n in range(2 * TG):
                    t.wait_ge(copied, TG + n - 1)
                    t.transpose(pt[(TG + n) % 2][:, 0:P], WV[:, n // TG, n % TG, :], ident[:, :]).then_inc(turned, 1)

            @block.vector
            def _(v):
                st = Steps(v, steps, pace["dve"])
                for j, A in enumerate((AS, AD)):
                    st.add(v.tensor_copy(parts[:, j, 0, :], A[:, :]))
                    st.last()
                    st.add(v.tensor_tensor(rest[:, j, :], A[:, :], parts[:, j, 0, :], ALU.subtract))
                    st.last()
                    st.add(v.tensor_copy(parts[:, j, 1, :], rest[:, j, :]))
                    st.last()
                    st.add(v.tensor_tensor(rest[:, j, :], rest[:, j, :], parts[:, j, 1, :], ALU.subtract))
                    st.last()
                    st.add(v.tensor_copy(parts[:, j, 2, :], rest[:, j, :]))
                st.add(v.memset(vals[:, :, :], 0.0))
                st.last()
                v.sem_inc(parts_ready, 1)
                v.wait_ge(consts, 1)
                for j in range(2):
                    blk = (blkS, blkD)[j]

                    def spread(i, h):
                        hold(v, low_in[h], i * 16 + 16 + j * (half // 2) * 16, pace["dve"])
                        if not (isinstance(i, int) and j == 0):
                            hold(v, r_done, i * 2 + h - 1 + j * half, pace["dve"])
                        v.tensor_scalar(LT[:, h, :], LR[:, h, :], pidx[:, :], None, ALU.is_equal)
                        v.tensor_tensor(OB[:, h, :, :],
                                        blk[:, bass.ds(i * (2 * GV) + h * GV, GV)].unsqueeze(2).to_broadcast([P, GV, NB]),
                                        io_b[:, :].unsqueeze(1).to_broadcast([P, GV, NB]),
                                        ALU.is_equal).then_inc(lt_ready, 1)

                    def pick(i, h):
                        hold(v, r_done, i * 2 + h + 1 + j * half, pace["dve"])
                        hold(v, lt_ready, i * 2 + h + 1 + j * half, pace["dve"])
                        v.tensor_tensor(R[:, h, :, :], pr[h][:, 0:GV * NB].rearrange("p (k b) -> p k b", b=NB),
                                        OB[:, h, :, :], ALU.mult).then_inc(picked, 1)
                        hold(v, picked, i * 2 + h + 1 + j * half, pace["dve"])
                        v.tensor_reduce(vals[:, j, bass.ds(i * (2 * GV) + h * GV, GV)], R[:, h, :, :], AX.X, ALU.add)

                    spread(0, 0)
                    with v.Fori(0, half // 2 - 1) as i:
                        spread(i, 1)
                        pick(i, 0)
                        spread(i + 1, 0)
                        pick(i, 1)
                    spread(half // 2 - 1, 1)
                    pick(half // 2 - 1, 0)
                    pick(half // 2 - 1, 1)
                st.add(v.memset(rw[:, 4, :], 0.0))
                st.last()
                st.add(v.tensor_tensor(z[:, :], vals[:, 0, :], vals[:, 1, :], ALU.add))
                st.last()
                v.scalar_tensor_tensor(z[:, :], z[:, :], SLOPE, z[:, :], ALU.mult, ALU.max).then_inc(z_ready, 1)
                for k in range(TG):
                    v.wait_ge(turned, k + 1)
                    v.tensor_copy(Z[:, k, :], pt[k % 2][:, 0:P]).then_inc(copied, 1)
                v.wait_ge(d_in, 16)
                st.add(v.tensor_copy(dF[:, :, :], dI[:, :, :]))
                st.last()
                st.add(v.memset(SF[:, :, :], -BIG))
                st.add(v.memset(SB[:, :, :], -BIG))
                st.add(v.tensor_tensor(FW[:, :, 1:P], dF[:, :, 1:P], dF[:, :, 0:P - 1], ALU.is_equal))
                st.last()
                st.add(v.tensor_scalar(SF[:, :, 1:P], FW[:, :, 1:P], -1.0, BIG, ALU.add, ALU.mult))
                st.add(v.tensor_scalar(SB[:, :, 0:P - 1], FW[:, :, 1:P], -1.0, BIG, ALU.add, ALU.mult))
                v.wait_ge(copied, TG)
                st.last()

                def flat(a):
                    return a[:, :, :].rearrange("p g e -> p (g e)")

                st.add(v.tensor_tensor_scan(flat(FW), flat(SF), flat(Z), -BIG, ALU.add, ALU.max))
                st.add(v.tensor_tensor_scan(flat(BW)[:, ::-1], flat(SB)[:, ::-1], flat(Z)[:, ::-1], -BIG,
                                            ALU.add, ALU.max))
                st.add(v.tensor_copy(e4[:, 0, :], dF[:, :, 0]))
                st.add(v.tensor_copy(e4[:, 1, :], dF[:, :, P - 1]))
                st.last()
                st.add(v.tensor_copy(e4[:, 2, :], FW[:, :, P - 1]))
                st.add(v.tensor_copy(e4[:, 3, :], BW[:, :, 0]))
                st.last()
                v.sem_inc(ends_ready, 1)
                v.wait_ge(moved, 80)
                first, last, fend, bend = (row[:, k, :] for k in range(4))
                one, cont, both, carry = rw[:, 2, :], rw[:, 3, :], rw[:, 5, :], rw[:, 4, :]
                st.add(v.memset(cont, -BIG))
                st.add(v.memset(carry, -BIG))
                st.add(v.memset(both, -BIG))
                st.add(v.memset(rw[:, 0:2, :], -BIG))
                st.add(v.tensor_tensor(one, first, last, ALU.is_equal))
                st.last()
                st.add(v.tensor_tensor(cont[:, 1:TP], first[:, 1:TP], last[:, 0:TP - 1], ALU.is_equal))
                st.last()
                st.add(v.tensor_scalar(cont[:, 1:TP], cont[:, 1:TP], -1.0, BIG, ALU.add, ALU.mult))
                st.add(v.tensor_scalar(one, one, -1.0, BIG, ALU.add, ALU.mult))
                st.last()
                st.add(v.tensor_tensor(both, cont, one, ALU.min))
                st.last()
                st.add(v.tensor_tensor_scan(carry, both, fend, -BIG, ALU.add, ALU.max))
                st.last()
                st.add(v.tensor_tensor(rw[:, 0, 1:TP], carry[:, 0:TP - 1], cont[:, 1:TP], ALU.add))
                st.last()
                st.add(v.memset(both[:, TP - 1:TP], -BIG))
                st.add(v.tensor_tensor(both[:, 0:TP - 1], cont[:, 1:TP], one[:, 0:TP - 1], ALU.min))
                st.last()
                st.add(v.tensor_tensor_scan(carry[:, ::-1], both[:, ::-1], bend[:, ::-1], -BIG, ALU.add, ALU.max))
                st.last()
                st.add(v.tensor_tensor(rw[:, 1, 0:TP - 1], carry[:, 1:TP], cont[:, 1:TP], ALU.add))
                st.last()
                v.sem_inc(carry_ready, 1)
                st.add(v.tensor_tensor(M[:, :, :], FW[:, :, :], BW[:, :, :], ALU.max))
                v.wait_ge(moved, 144)
                for k, end in ((0, 0), (1, P - 1)):
                    st.last()
                    st.add(v.tensor_tensor(SF[:, :, :], dF[:, :, :],
                                           dF[:, :, end:end + 1].to_broadcast([P, TG, P]), ALU.is_equal))
                    st.last()
                    st.add(v.tensor_scalar(SF[:, :, :], SF[:, :, :], -1.0, BIG, ALU.add, ALU.mult))
                    st.last()
                    st.add(v.tensor_tensor(SF[:, :, :], SF[:, :, :],
                                           cr[:, k, :].unsqueeze(2).to_broadcast([P, TG, P]), ALU.add))
                    st.last()
                    st.add(v.tensor_tensor(M[:, :, :], M[:, :, :], SF[:, :, :], ALU.max))
                st.last()
                v.tensor_tensor(Z[:, :, :], Z[:, :, :], M[:, :, :], ALU.subtract).then_inc(e_ready, 1)
                for n in range(2 * TG):
                    v.wait_ge(turned, TG + n + 1)
                    to = (WE if n < TG else ME)[:, (n % TG) * P:(n % TG + 1) * P]
                    v.tensor_copy(to, pt[(TG + n) % 2][:, 0:P]).then_inc(copied, 1)
                v.wait_ge(copied, 3 * TG)
                v.memset(ACC[:, :], 0.0)

        aggregate("e_", table2, True)

        edges.close()
        sb, pb, sem = mk(ctx)
        wgt = sb("wgt", [P, 3, NB])

        with ExitStack() as sc:
            sb, pb, sem = mk(sc)
            s1 = sb("f_s1", [P, 10, NB])
            brow = sb("f_brow", [P, 2, D])
            T0 = sb("f_T0", [P, 2, D])
            XT = sb("f_XT", [P, 2, 2, P])
            XW = sb("f_XW", [P, 2, D])
            XR = sb("f_XR", [P, 2, D])
            U = sb("f_U", [P, 2, D])
            blank = sb("f_blank", [P, W])
            blanked = sem("f_blanked")
            blank_out = sem("f_blank_out")
            stats = sb("f_stats", [P, NB * 6])
            sm = sb("f_sm", [P, 2, NB])
            mean = sb("f_mean", [P, NB])
            rstd = sb("f_rstd", [P, NB])
            pt = [pb(f"f_pt{i}", [P, 512]) for i in range(2)]
            pm = [pb(f"f_pm{i}", [P, 512]) for i in range(2)]
            w_in = sem("f_w_in")
            exps = sem("f_exps")
            exped = sem("f_exped")
            rows_in = [sem("f_rows_in0"), sem("f_rows_in1")]
            taken = sem("f_taken")
            turned = sem("f_turned")
            xt_ready = sem("f_xt_ready")
            mixed = sem("f_mixed")
            summed = sem("f_summed")
            root_in = sem("f_root_in")
            root_out = sem("f_root_out")
            steps = sem("f_steps")
            fs = sem("f_fs")
            block = sc.enter_context(nc.Block())

            @block.sync
            def _(sp):
                sp.dma_start(brow[:, 0, :], gb2.partition_broadcast(P)).then_inc(w_in, 16)
                sp.dma_start(brow[:, 1, :], b_out.partition_broadcast(P)).then_inc(w_in, 16)

                sp.wait_ge(blanked, 2)
                sp.dma_start(XS.rearrange("(t p) c -> p t c", p=P), blank[:, :].unsqueeze(1).to_broadcast([P, NTL, W])
                             ).then_inc(blank_out, 16)

                def load(n, par):
                    if not isinstance(n, int) or n >= 2:
                        hold(sp, summed, n - 1, pace["sp"])
                    sp.dma_start(XW[:, par, :], table2[bass.ds(n * P, P), :]).then_inc(rows_in[par], 16)
                    sp.dma_start(XR[:, par, :], x_pad[bass.ds(n * P, P), :]).then_inc(rows_in[par], 16)

                skewed(sp, [load])
                sp.wait_ge(blank_out, 16)

            @block.gpsimd
            def _(g):
                g.memset(blank[:, :], 0.0).then_inc(blanked, 1)
                g.wait_ge(blanked, 1)
                g.memset(blank[:, D:D + 1], float(1 << 20)).then_inc(blanked, 1)

            @block.scalar
            def _(a):
                a.wait_ge(exps, 1)
                a.activation(s1[:, 4:6, :], s1[:, 2:4, :], ACT.Exp).then_inc(exped, 1)

                def take(n, par):
                    reuse(a, turned, n, pace["act"])
                    a.copy(T0[:, par, :], X[:, bass.ds(n * XP, D)]).then_inc(taken, 1)

                def xt(n, par):
                    hold(a, turned, n + 1, pace["act"])
                    reuse(a, mixed, n, pace["act"])
                    a.copy(XT[:, par, :, :], pt[par][:, 0:D].rearrange("p (k q) -> p k q", k=2)).then_inc(xt_ready, 1)

                skewed(a, [take, xt])
                a.wait_ge(root_in, 1)
                a.activation(sm[:, 1, :], sm[:, 0, :], ACT.Sqrt).then_inc(root_out, 1)

            @block.tensor
            def _(t):
                def turn(n, par):
                    hold(t, taken, n + 1, pace["pe"])
                    reuse(t, xt_ready, n, pace["pe"])
                    for k in range(2):
                        ins = t.transpose(pt[par][:, k * P:(k + 1) * P], T0[:, par, k * P:(k + 1) * P], ident[:, :])
                    ins.then_inc(turned, 1)

                def mix(n, par):
                    hold(t, xt_ready, n + 1, pace["pe"])
                    reuse(t, summed, n, pace["pe"])
                    for k in range(2):
                        ins = t.matmul(pm[par][:, 0:D], XT[:, par, k, :], MX[:, k, :], start=(k == 0), stop=(k == 1))
                    ins.then_inc(mixed, 1)

                skewed(t, [turn, mix])

            @block.vector
            def _(v):
                st = Steps(v, steps, pace["dve"])
                ssum, qsum = Ab[:, :, D], Ab[:, :, D + 1]
                st.add(v.tensor_tensor(s1[:, 0, :], AS[:, :], AD[:, :], ALU.add))
                st.add(v.tensor_scalar(s1[:, 1, :], ssum, 0.5, None, ALU.is_lt))
                st.last()
                st.add(v.scalar_tensor_tensor(s1[:, 0, :], s1[:, 0, :], SLOPE, s1[:, 0, :], ALU.mult, ALU.max))
                st.add(v.tensor_tensor(s1[:, 2, :], ssum, s1[:, 1, :], ALU.add))
                st.last()
                st.add(v.reciprocal(s1[:, 3, :], s1[:, 2, :]))
                st.last()
                st.add(v.tensor_tensor(s1[:, 2, :], qsum, s1[:, 3, :], ALU.mult))
                st.last()
                st.add(v.scalar_tensor_tensor(s1[:, 2, :], s1[:, 1, :], -BIG, s1[:, 2, :], ALU.mult, ALU.add))
                st.last()
                st.add(v.tensor_tensor(s1[:, 6, :], s1[:, 2, :], s1[:, 0, :], ALU.max))
                st.last()
                st.add(v.tensor_tensor(s1[:, 2, :], s1[:, 2, :], s1[:, 6, :], ALU.subtract))
                st.add(v.tensor_tensor(s1[:, 3, :], s1[:, 0, :], s1[:, 6, :], ALU.subtract))
                st.last()
                v.sem_inc(exps, 1)
                v.wait_ge(exped, 1)
                st.add(v.tensor_tensor(s1[:, 7, :], s1[:, 4, :], ssum, ALU.mult))
                st.last()
                st.add(v.scalar_tensor_tensor(s1[:, 7, :], s1[:, 7, :], 1e-16, s1[:, 5, :], ALU.add, ALU.add))
                st.last()
                st.add(v.reciprocal(s1[:, 8, :], s1[:, 7, :]))
                st.last()
                st.add(v.tensor_tensor(wgt[:, 0, :], s1[:, 4, :], s1[:, 8, :], ALU.mult))
                st.add(v.tensor_tensor(wgt[:, 1, :], s1[:, 5, :], s1[:, 8, :], ALU.mult))
                st.last()
                v.wait_ge(w_in, 32)

                def total(n, par):
                    acc, u = ACC[:, bass.ds(n * W, D)], U[:, par, :]

                    def step(k, ins):
                        ins.then_inc(fs, 1)
                        hold(v, fs, n * 5 + k + 1, pace["dve"])

                    hold(v, rows_in[par], n * 16 + (32 if par == 0 else 16), pace["dve"])
                    step(0, v.tensor_scalar(u, acc, wgt[:, 0, bass.ds(n, 1)], None, ALU.mult))
                    step(1, v.scalar_tensor_tensor(u, XW[:, par, :], wgt[:, 1, bass.ds(n, 1)], u, ALU.mult, ALU.add))
                    step(2, v.tensor_tensor(u, u, brow[:, 0, :], ALU.add))
                    step(3, v.scalar_tensor_tensor(u, u, 0.0, XR[:, par, :], ALU.max, ALU.add))
                    hold(v, mixed, n + 1, pace["dve"])
                    step(4, v.tensor_tensor(u, u, pm[par][:, 0:D], ALU.add))
                    v.tensor_tensor(acc, u, brow[:, 1, :], ALU.add).then_inc(summed, 1)

                skewed(v, [lambda n, par: None, total])
                v.wait_ge(summed, NB)
                layernorm(v, st, ACC, W, X, stats, sm, mean[:, :], rstd[:, :], root_in, root_out)

        g_all = ctx.enter_context(ExitStack())
        sb, pb, sem = mk(g_all)
        F1 = sb("g_F1", [P, 2, NE * HID])
        F2 = sb("g_F2", [P, NE * HC * D])
        ev = sb("g_ev", [1, P], I32)
        ffn_in = sem("g_ffn_in")
        with ExitStack() as sc:
            sb, pb, sem = mk(sc)
            GW = sb("g_GW", [P, 2, NE])
            GB = sb("g_GB", [1, NE])
            ones = sb("g_ones", [P, P])
            upper = sb("g_upper", [P, P])
            T0 = sb("g_T0", [P, 2, D])
            XT = sb("g_XT", [P, 2, 2, P])
            SC = sb("g_SC", [P, NB, NE])
            C1 = sb("g_C1", [P, GB_STEP, NE, NE])
            C2 = sb("g_C2", [P, GB_STEP, NE, NE])
            tri = sb("g_tri", [P, NE, NE])
            MK = sb("g_MK", [P, NB, NE])
            TE = sb("g_TE", [P, NE, NB])
            CE = sb("g_CE", [P, NE, NB])
            cnt = sb("g_cnt", [P, 4, NE])
            cntI = sb("g_cntI", [P, NE], I32)
            token = sb("g_token", [P, NB])
            pos = sb("g_pos", [P, 2, NB])
            posI = sb("g_posI", [P, 2, NB], I32)
            evf = sb("g_evf", [1, P])
            nil = sb("g_nil", [P, NB])
            pt = [pb(f"g_pt{i}", [P, 512]) for i in range(2)]
            pg = [pb(f"g_pg{i}", [P, 512]) for i in range(2)]
            pc = [pb(f"g_pc{i}", [P, 512]) for i in range(2)]
            w_in = sem("g_w_in")
            consts = sem("g_consts")
            taken = sem("g_taken")
            turned = sem("g_turned")
            xt_ready = sem("g_xt_ready")
            gated = sem("g_gated")
            sc_ready = sem("g_sc_ready")
            mk_ready = sem("g_mk_ready")
            counted = sem("g_counted")
            placed = sem("g_placed")
            scattered = sem("g_scattered")
            steps = sem("g_steps")
            block = sc.enter_context(nc.Block())

            @block.sync
            def _(sp):
                sp.dma_start(GW[:, :, :], Wg.rearrange("(k p) e -> p k e", p=P)).then_inc(w_in, 16)
                sp.dma_start(GB[:, :], bg.unsqueeze(0)).then_inc(w_in, 16)
                for k in range(2):
                    sp.dma_start(F1[:, k, :].rearrange("p (e h) -> p e h", h=HID),
                                 fW1[:, k * P:(k + 1) * P, :].rearrange("e p h -> p e h")).then_inc(ffn_in, 16)
                sp.dma_start(F2[:, :].rearrange("p (c d) -> p c d", d=D),
                             fW2.rearrange("e h d -> (e h) d").rearrange("(c p) d -> p c d", p=P)).then_inc(ffn_in, 16)
                sp.wait_ge(ffn_in, 48)

            @block.gpsimd
            def _(g):
                g.memset(tri[:, :, :], 1.0).then_inc(consts, 1)
                g.memset(ones[:, :], 1.0).then_inc(consts, 1)
                g.memset(upper[:, :], 1.0).then_inc(consts, 1)
                g.iota(token[:, :], [[P, NB]], base=0, channel_multiplier=1,
                       allow_small_or_imprecise_dtypes=True).then_inc(consts, 1)
                g.wait_ge(consts, 4)
                g.affine_select(out=tri[:, :, :], in_=tri[:, :, :], compare_op=ALU.is_gt, fill=0.0,
                                base=0, pattern=[[-1, NE], [1, NE]], channel_multiplier=0).then_inc(consts, 1)
                g.affine_select(out=upper[:, :], in_=upper[:, :], compare_op=ALU.is_gt, fill=0.0,
                                base=0, pattern=[[1, P]], channel_multiplier=-1).then_inc(consts, 1)
                g.wait_ge(placed, 1)
                for b in range(NB):
                    for k in range(2):
                        g.indirect_dma_start(XS[:, :], bass.IndirectOffsetOnAxis(ap=posI[:, k, b:b + 1], axis=0),
                                             Xb[:, b, :], None).then_inc(scattered, 16)
                g.wait_ge(scattered, 2 * NB * 16)

            @block.scalar
            def _(a):
                def take(n, par):
                    reuse(a, turned, n, pace["act"])
                    a.copy(T0[:, par, :], X[:, bass.ds(n * XP, D)]).then_inc(taken, 1)

                def xt(n, par):
                    hold(a, turned, n + 1, pace["act"])
                    reuse(a, gated, n, pace["act"])
                    a.copy(XT[:, par, :, :], pt[par][:, 0:D].rearrange("p (k q) -> p k q", k=2)).then_inc(xt_ready, 1)

                skewed(a, [take, xt])

            @block.tensor
            def _(t):
                t.wait_ge(w_in, 32)
                t.wait_ge(consts, 6)

                def turn(n, par):
                    hold(t, taken, n + 1, pace["pe"])
                    reuse(t, xt_ready, n, pace["pe"])
                    for k in range(2):
                        ins = t.transpose(pt[par][:, k * P:(k + 1) * P], T0[:, par, k * P:(k + 1) * P], ident[:, :])
                    ins.then_inc(turned, 1)

                def gate(n, par):
                    hold(t, xt_ready, n + 1, pace["pe"])
                    reuse(t, sc_ready, n, pace["pe"])
                    t.matmul(pg[par][:, 0:NE], ones[0:1, :], GB[:, :], start=True, stop=False)
                    for k in range(2):
                        ins = t.matmul(pg[par][:, 0:NE], XT[:, par, k, :], GW[:, k, :], start=False, stop=(k == 1))
                    ins.then_inc(gated, 1)

                skewed(t, [turn, gate])
                t.wait_ge(mk_ready, 1)
                mask = MK[:, :, :].rearrange("p b e -> p (b e)")
                t.matmul(pc[0][:, 0:NB * NE], upper[:, :], mask, start=True, stop=True).then_inc(counted, 1)
                t.matmul(pc[1][:, 0:NB * NE], ones[:, :], mask, start=True, stop=True).then_inc(counted, 1)

            @block.vector
            def _(v):
                st = Steps(v, steps, pace["dve"])

                def score(n, par):
                    hold(v, gated, n + 1, pace["dve"])
                    v.tensor_copy(SC[:, bass.ds(n, 1), :], pg[par][:, 0:NE].unsqueeze(1)).then_inc(sc_ready, 1)

                skewed(v, [lambda n, par: None, score])
                v.wait_ge(sc_ready, NB)
                v.wait_ge(consts, 6)
                full = [P, GB_STEP, NE, NE]
                for b in range(0, NB, GB_STEP):
                    s = SC[:, b:b + GB_STEP, :]
                    other, mine = s.unsqueeze(3).to_broadcast(full), s.unsqueeze(2).to_broadcast(full)
                    st.add(v.tensor_tensor(C1[:, :, :, :], other, mine, ALU.is_gt))
                    st.add(v.tensor_tensor(C2[:, :, :, :], other, mine, ALU.is_equal))
                    st.last()
                    c2 = C2[:, :, :, :].rearrange("p b i j -> p b (i j)")
                    st.add(v.tensor_tensor(c2, c2, tri[:, :, :].rearrange("p i j -> p (i j)").unsqueeze(1)
                                           .to_broadcast([P, GB_STEP, NE * NE]), ALU.mult))
                    st.last()
                    st.add(v.tensor_tensor(C1[:, :, :, :], C1[:, :, :, :], C2[:, :, :, :], ALU.add))
                    st.last()
                    st.add(v.tensor_reduce(MK[:, b:b + GB_STEP, :], C1[:, :, :, :].rearrange("p b i j -> p b j i"),
                                           AX.X, ALU.add))
                    st.last()
                st.add(v.tensor_scalar(MK[:, :, :], MK[:, :, :], 1.5, None, ALU.is_lt))
                st.last()
                v.sem_inc(mk_ready, 1)
                v.wait_ge(counted, 2)
                st.add(v.tensor_copy(TE[:, :, :], pc[1][:, 0:NB * NE].rearrange("p (b e) -> p e b", e=NE)))
                st.add(v.memset(cnt[:, 3, :], 0.0))
                st.last()
                st.add(v.tensor_reduce(cnt[:, 0, :], TE[:, :, :], AX.X, ALU.add))
                st.last()
                st.add(v.tensor_scalar(cntI[:, :], cnt[:, 0, :], float(P - 1), None, ALU.add))
                st.last()
                st.add(v.tensor_scalar(cntI[:, :], cntI[:, :], 7, None, ALU.arith_shift_right))
                st.last()
                st.add(v.tensor_copy(cnt[:, 1, :], cntI[:, :]))
                st.last()
                st.add(v.tensor_tensor_scan(cnt[:, 2, :], cnt[:, 1, :], cnt[:, 3, :], 0.0, ALU.add, ALU.add))
                st.last()
                st.add(v.tensor_tensor(cnt[:, 2, :], cnt[:, 2, :], cnt[:, 1, :], ALU.subtract))
                st.last()
                st.add(v.memset(evf[:, :], 0.0))
                for e in range(1, NE):
                    st.last()
                    st.add(v.scalar_tensor_tensor(evf[:, :], iota_f[0:1, :], cnt[0:1, 2, e:e + 1], evf[:, :],
                                                  ALU.is_ge, ALU.add))
                st.last()
                st.add(v.tensor_copy(ev[:, :], evf[:, :]))
                st.add(v.tensor_scalar(cnt[:, 3, :], cnt[:, 2, :], float(P), None, ALU.mult))
                st.add(v.memset(nil[:, :], 0.0))
                st.last()
                for e in range(NE):
                    st.add(v.tensor_tensor_scan(CE[:, e, :], TE[:, e, :], nil[:, :],
                                                cnt[:, 3, e:e + 1], ALU.add, ALU.add))
                st.last()
                st.add(v.tensor_tensor(CE[:, :, :], CE[:, :, :], TE[:, :, :], ALU.subtract))
                st.last()
                places = SC
                st.add(v.tensor_tensor(places[:, :, :], pc[0][:, 0:NB * NE].rearrange("p (b e) -> p b e", e=NE),
                                       CE[:, :, :].rearrange("p e b -> p b e"), ALU.add))
                st.last()
                far = float(1 << 20)
                ms = TE[:, :, :].rearrange("p e b -> p (e b)").rearrange("p (b e) -> p b e", e=NE)
                st.add(v.tensor_scalar(ms, MK[:, :, :], -far, far, ALU.mult, ALU.add))
                st.last()
                st.add(v.tensor_tensor(ms, ms, places[:, :, :], ALU.add))
                st.add(v.tensor_tensor(places[:, :, :], places[:, :, :], MK[:, :, :], ALU.mult))
                st.last()
                st.add(v.tensor_reduce(pos[:, 0, :], ms, AX.X, ALU.min))
                st.add(v.tensor_reduce(pos[:, 1, :], places[:, :, :], AX.X, ALU.max))
                st.last()
                st.add(v.tensor_copy(posI[:, :, :], pos[:, :, :]))
                st.add(v.tensor_copy(Xb[:, :, D], token[:, :]))
                st.add(v.tensor_copy(Xb[:, :, D + 1], pos[:, 0, :]))
                st.last()
                v.sem_inc(placed, 1)

        with ExitStack() as sc:
            sb, pb, sem = mk(sc)
            B1 = sb("h_B1", [P, NE * HID])
            B2 = sb("h_B2", [P, NE * D])
            XR = sb("h_XR", [P, 2, W])
            XT = sb("h_XT", [P, 2, 2, P])
            HB = sb("h_HB", [P, 2, HID])
            HS = HB
            HT = sb("h_HT", [P, 2, HID])
            Y = sb("h_Y", [P, 2, D])
            place = sb("h_place", [P, 1])
            own = sb("h_own", [P, 4])
            to = sb("h_to", [P, 2], I32)
            later = sb("h_later", [P, 3, 2])
            px = [pb(f"h_px{i}", [P, 512]) for i in range(2)]
            p1 = [pb(f"h_p1{i}", [P, 512]) for i in range(2)]
            p2 = [pb(f"h_p2{i}", [P, 512]) for i in range(2)]
            p3 = [pb(f"h_p3{i}", [P, 512]) for i in range(2)]
            b_in = sem("h_b_in")
            consts = sem("h_consts")
            rows_in = [sem("h_rows_in0"), sem("h_rows_in1")]
            turned = sem("h_turned")
            xt_ready = sem("h_xt_ready")
            h_done = sem("h_h_done")
            hb_ready = sem("h_hb_ready")
            hs_ready = sem("h_hs_ready")
            h_turned = sem("h_h_turned")
            ht_ready = sem("h_ht_ready")
            y_done = sem("h_y_done")
            y_ready = sem("h_y_ready")
            to_ready = sem("h_to_ready")
            ids = sem("h_ids")
            kept = sem("h_kept")
            kept2 = sem("h_kept2")
            kept3 = sem("h_kept3")
            sent = [sem("h_sent0"), sem("h_sent1")]
            block = sc.enter_context(nc.Block())

            @block.sync
            def _(sp):
                sp.dma_start(B1[:, :], fb1.rearrange("e h -> (e h)").partition_broadcast(P)).then_inc(b_in, 16)
                sp.dma_start(B2[:, :], fb2.rearrange("e h -> (e h)").partition_broadcast(P)).then_inc(b_in, 16)

                def load(n, par):
                    reuse(sp, turned, n, pace["sp"])
                    reuse(sp, to_ready, n, pace["sp"])
                    sp.dma_start(XR[:, par, :], XS[bass.ds(n * P, P), :]).then_inc(rows_in[par], 16)

                skewed(sp, [load], NTL)

            @block.gpsimd
            def _(g):
                g.iota(place[:, :], [[0, 1]], base=0, channel_multiplier=1,
                       allow_small_or_imprecise_dtypes=True).then_inc(consts, 1)

                def send(n, par):
                    hold(g, kept3, n + 1, pace["pool"])
                    hold(g, y_ready, n + 1, pace["pool"])
                    g.indirect_dma_start(YS[:, :], bass.IndirectOffsetOnAxis(ap=to[:, par:par + 1], axis=0),
                                         Y[:, par, :], None).then_inc(sent[par], 16)

                skewed(g, [send], NTL)
                for k in range(2):
                    g.wait_ge(sent[k], NTL // 2 * 16)

            @block.scalar
            def _(a):
                def xt(n, par):
                    hold(a, turned, n + 1, pace["act"])
                    reuse(a, h_done, n, pace["act"])
                    a.copy(XT[:, par, :, :], px[par][:, 0:D].rearrange("p (k q) -> p k q", k=2)).then_inc(xt_ready, 1)

                def gelu(n, par):
                    hold(a, hb_ready, n + 1, pace["act"])
                    a.activation(HS[:, par, :], HB[:, par, :], ACT.Gelu).then_inc(hs_ready, 1)

                skewed(a, [xt, gelu], NTL)

            @block.tensor
            def _(t):
                reg1 = t.alloc_register(name="expert_up")
                reg2 = t.alloc_register(name="expert_down")

                def turn(n, par):
                    hold(t, rows_in[par], n * 8 + (16 if par == 0 else 8), pace["pe"])
                    reuse(t, xt_ready, n, pace["pe"])
                    for k in range(2):
                        ins = t.transpose(px[par][:, k * P:(k + 1) * P], XR[:, par, k * P:(k + 1) * P], ident[:, :])
                    ins.then_inc(turned, 1)

                def up(n, par):
                    t.load(reg1, ev[0:1, bass.ds(n, 1)])
                    e = t.snap(reg1, min_val=0, max_val=NE - 1)
                    hold(t, xt_ready, n + 1, pace["pe"])
                    reuse(t, hb_ready, n, pace["pe"])
                    for k in range(2):
                        ins = t.matmul(p1[par][:, :], XT[:, par, k, :], F1[:, k, bass.ds(e * HID, HID)],
                                       start=(k == 0), stop=(k == 1))
                    ins.then_inc(h_done, 1)

                def turn_h(n, par):
                    hold(t, hs_ready, n + 1, pace["pe"])
                    reuse(t, ht_ready, n, pace["pe"])
                    for c in range(HC):
                        ins = t.transpose(p2[par][:, c * P:(c + 1) * P], HS[:, par, c * P:(c + 1) * P], ident[:, :])
                    ins.then_inc(h_turned, 1)

                def down(n, par):
                    t.load(reg2, ev[0:1, bass.ds(n, 1)])
                    e = t.snap(reg2, min_val=0, max_val=NE - 1)
                    hold(t, ht_ready, n + 1, pace["pe"])
                    reuse(t, y_ready, n, pace["pe"])
                    for c in range(HC):
                        ins = t.matmul(p3[par][:, 0:D], HT[:, par, c * P:(c + 1) * P],
                                       F2[:, bass.ds(e * (HC * D) + c * D, D)], start=(c == 0), stop=(c == HC - 1))
                    ins.then_inc(y_done, 1)

                skewed(t, [turn, up, turn_h, down], NTL)

            @block.vector
            def _(v):
                reg1 = v.alloc_register(name="expert_b1")
                reg2 = v.alloc_register(name="expert_b2")
                v.wait_ge(consts, 1)
                v.wait_ge(b_in, 32)

                def target(n, par):
                    hold(v, rows_in[par], n * 8 + (16 if par == 0 else 8), pace["dve"])
                    if isinstance(n, int):
                        v.memset(own[:, 3:4], float(n * P)).then_inc(ids, 1)
                    else:
                        v.tensor_scalar(own[:, 3:4], own[:, 3:4], float(P), None, ALU.add).then_inc(ids, 1)
                    hold(v, ids, n * 4 + 1, pace["dve"])
                    v.tensor_tensor(own[:, 0:1], place[:, :], own[:, 3:4], ALU.add).then_inc(ids, 1)
                    hold(v, ids, n * 4 + 2, pace["dve"])
                    v.tensor_tensor(own[:, 1:2], own[:, 0:1], XR[:, par, D + 1:D + 2], ALU.not_equal).then_inc(ids, 1)
                    hold(v, ids, n * 4 + 3, pace["dve"])
                    v.scalar_tensor_tensor(own[:, 2:3], own[:, 1:2], float(NP), XR[:, par, D:D + 1], ALU.mult,
                                           ALU.add).then_inc(ids, 1)
                    hold(v, ids, n * 4 + 4, pace["dve"])
                    reuse(v, kept, n, pace["dve"])
                    v.scalar_tensor_tensor(later[:, 0, par:par + 1], own[:, 0:1], float(2 * NP), own[:, 2:3], ALU.add,
                                           ALU.min).then_inc(to_ready, 1)

                def hand_on(n, par, j):
                    hold(v, (to_ready, kept)[j - 1], n + 1, pace["dve"])
                    reuse(v, (kept2, kept3)[j - 1], n, pace["dve"])
                    v.tensor_copy(later[:, j, par:par + 1], later[:, j - 1, par:par + 1]).then_inc((kept, kept2)[j - 1], 1)

                def bias_h(n, par):
                    hand_on(n, par, 1)
                    v.load(reg1, ev[0:1, bass.ds(n, 1)])
                    e = v.snap(reg1, min_val=0, max_val=NE - 1)
                    hold(v, h_done, n + 1, pace["dve"])
                    reuse(v, h_turned, n, pace["dve"])
                    v.tensor_tensor(HB[:, par, :], p1[par][:, :], B1[:, bass.ds(e * HID, HID)], ALU.add
                                    ).then_inc(hb_ready, 1)

                def keep_h(n, par):
                    hand_on(n, par, 2)
                    hold(v, h_turned, n + 1, pace["dve"])
                    reuse(v, y_done, n, pace["dve"])
                    v.tensor_copy(HT[:, par, :], p2[par][:, :]).then_inc(ht_ready, 1)

                def bias_y(n, par):
                    v.load(reg2, ev[0:1, bass.ds(n, 1)])
                    e = v.snap(reg2, min_val=0, max_val=NE - 1)
                    hold(v, y_done, n + 1, pace["dve"])
                    if not isinstance(n, int) or n >= 2:
                        hold(v, sent[par], n * 8 - (0 if par == 0 else 8), pace["dve"])
                    hold(v, kept2, n + 1, pace["dve"])
                    v.tensor_copy(to[:, par:par + 1], later[:, 2, par:par + 1]).then_inc(kept3, 1)
                    v.tensor_tensor(Y[:, par, :], p3[par][:, 0:D], B2[:, bass.ds(e * D, D)], ALU.add
                                    ).then_inc(y_ready, 1)

                skewed(v, [target, bias_h, keep_h, bias_y], NTL)

        with ExitStack() as sc:
            sb, pb, sem = mk(sc)
            YB = sb("i_YB", [P, 2, 2, TB * D])
            y_in = [sem("i_y_in0"), sem("i_y_in1")]
            half = sem("i_half")
            added = sem("i_added")
            stored = sem("i_stored")
            block = sc.enter_context(nc.Block())
            ng = NB // TB

            @block.sync
            def _(sp):
                def load(n, par):
                    reuse(sp, added, n, pace["sp"])
                    for k in range(2):
                        sp.dma_start(YB[:, par, k, :].rearrange("p (b d) -> p b d", d=D),
                                     YS[bass.ds(n * TT + k * NP, TT), :].rearrange("(b l) d -> l b d", l=P)
                                     ).then_inc(y_in[par], 16)

                skewed(sp, [load], ng)

            @block.scalar
            def _(a):
                def store(n, par):
                    hold(a, added, n + 1, pace["act"])
                    a.dma_start(out[bass.ds(n * TT, TT), :].rearrange("(b l) d -> l b d", l=P),
                                ACC[:, bass.ds(n * (TB * W), TB * W)].rearrange("p (b c) -> p b c", c=W)[:, :, 0:D]
                                ).then_inc(stored, 16)

                with a.Fori(0, ng - 1) as i:
                    store(i, 0)
                a.wait_ge(added, ng)
                last = NB - TB
                a.dma_start(out[last * P:FULL * P, :].rearrange("(b l) d -> l b d", l=P),
                            Ab[:, last:FULL, 0:D]).then_inc(stored, 16)
                a.dma_start(out[FULL * P:N, :], Ab[0:REST, FULL, 0:D]).then_inc(stored, 16)
                a.wait_ge(stored, 16 * (ng + 1))

            @block.vector
            def _(v):
                def add(n, par):
                    acc = ACC[:, bass.ds(n * (TB * W), TB * W)].rearrange("p (b c) -> p b c", c=W)[:, :, 0:D]
                    hold(v, y_in[par], n * 16 + (32 if par == 0 else 16), pace["dve"])
                    v.tensor_tensor(acc, acc, YB[:, par, 0, :].rearrange("p (b d) -> p b d", d=D), ALU.add
                                    ).then_inc(half, 1)
                    hold(v, half, n + 1, pace["dve"])
                    v.tensor_tensor(acc, acc, YB[:, par, 1, :].rearrange("p (b d) -> p b d", d=D), ALU.add
                                    ).then_inc(added, 1)

                skewed(v, [add], ng)

_INS = ['x', 'src', 'dst', 'L0_gnn_W1', 'L0_gnn_b1', 'L0_gnn_W2', 'L0_gnn_att_src', 'L0_gnn_att_dst', 'L0_gnn_b2',
        'L0_mix_w_qkv', 'L0_mix_w_out', 'L0_mix_b_out', 'L0_ffn_Wg', 'L0_ffn_bg', 'L0_ffn_W1', 'L0_ffn_b1',
        'L0_ffn_W2', 'L0_ffn_b2']


def kernel(**inputs):
    import numpy as np
    import concourse.bacc as bacc
    from concourse.bass_utils import run_bass_kernel_spmd as run

    nc = bacc.Bacc("TRN2", target_bir_lowering=False, num_devices=1)
    arrays, args = {}, []
    for name in _INS:
        a = np.ascontiguousarray(inputs[name])
        arrays["in_" + name] = a
        args.append(nc.dram_tensor("in_" + name, a.shape, mybir.dt.from_np(a.dtype), kind="ExternalInput").ap())
    o = nc.dram_tensor("out_0", (N, D), F32, kind="ExternalOutput").ap()
    program(nc, *args, o)
    r = run(nc, [arrays], core_ids=[0])
    return r.results[0]["out_0"]
```
